# Optimizing a Trainium2 kernel written in Bass

```python
import numpy as np
import jax
import jax.numpy as jnp

def _softmax(x, axis=-1):
    return jax.nn.softmax(x, axis=axis)

def _gelu(x):
    return jax.nn.gelu(x, approximate=True)

def _silu(x):
    return jax.nn.silu(x)

def _sigmoid(x):
    return jax.nn.sigmoid(x)

def _layernorm(x, axis=-1, eps=1e-05):
    m = jnp.mean(x, axis=axis, keepdims=True)
    v = jnp.var(x, axis=axis, keepdims=True)
    return (x - m) / jnp.sqrt(v + eps)

def _scatter_add(tgt, idx, src, axis=0):
    return tgt.at[idx].add(src)

def _segment_sum(src, seg, n):
    return jax.ops.segment_sum(src, seg, n)
kernel_name = 'mk_seq_preln_d1_jaxref_r2_1cf509'

def setup_inputs(seed: int=0):
    np.random.seed(seed)
    _w = jnp.asarray

    def _L0_attn_setup():
        import jax, jax.numpy as jnp
        import numpy as np
        key = jax.random.key(seed)
        ks = jax.random.split(key, 5)
        B, S, D = (2, 1024, 512)
        scale = 0.02
        return {'x': jax.random.normal(ks[0], (B, S, D), dtype=jnp.float32), 'q_proj_weight': jax.random.normal(ks[1], (D, D), dtype=jnp.float32) * scale, 'k_proj_weight': jax.random.normal(ks[2], (D, D), dtype=jnp.float32) * scale, 'v_proj_weight': jax.random.normal(ks[3], (D, D), dtype=jnp.float32) * scale, 'o_proj_weight': jax.random.normal(ks[4], (D, D), dtype=jnp.float32) * scale}
    _L0_attn_in = _L0_attn_setup()

    def _L0_ffn_setup():
        import jax, jax.numpy as jnp
        import numpy as np
        FP8_MAX = 448.0

        def quant_fp8(x):
            amax = jnp.max(jnp.abs(x)).astype(jnp.float32)
            scale = jnp.minimum(FP8_MAX / jnp.maximum(amax, 1e-12), FP8_MAX)
            x_fp8 = jnp.clip(x * scale, -FP8_MAX, FP8_MAX).astype(jnp.float8_e4m3fn)
            return (x_fp8, 1.0 / scale)
        key = jax.random.key(seed)
        k1, k2, k3 = jax.random.split(key, 3)
        B, S, IN, OUT = (4, 4096, 512, 512)
        input = jax.random.normal(k1, (B, S, IN), dtype=jnp.float32)
        bound = 1.0 / np.sqrt(IN)
        weight = jax.random.uniform(k2, (OUT, IN), dtype=jnp.float32, minval=-bound, maxval=bound)
        bias = jax.random.uniform(k3, (OUT,), dtype=jnp.float32, minval=-bound, maxval=bound)
        return {'input': input, 'weight': weight, 'bias': bias}
    _L0_ffn_in = _L0_ffn_setup()
    _d = {'L0_attn_x': _L0_attn_in['x'], 'L0_attn_q_proj_weight': _L0_attn_in['q_proj_weight'], 'L0_attn_k_proj_weight': _L0_attn_in['k_proj_weight'], 'L0_attn_v_proj_weight': _L0_attn_in['v_proj_weight'], 'L0_attn_o_proj_weight': _L0_attn_in['o_proj_weight'], 'L0_ffn_weight': _L0_ffn_in['weight'], 'L0_ffn_bias': _L0_ffn_in['bias']}
    _x0 = _d['L0_attn_x']
    _d['L0_attn_x'] = jax.random.normal(jax.random.fold_in(jax.random.key(seed), 1), (8, 1024, 512), dtype=_x0.dtype)
    del _x0
    return _d

def reference(L0_attn_x, L0_attn_q_proj_weight, L0_attn_k_proj_weight, L0_attn_v_proj_weight, L0_attn_o_proj_weight, L0_ffn_weight, L0_ffn_bias):

    def _L0_attn_ref(x, q_proj_weight, k_proj_weight, v_proj_weight, o_proj_weight):
        import jax, jax.numpy as jnp
        import numpy as np
        num_heads = 16
        B, S, d_in = x.shape
        d_k = q_proj_weight.shape[0]
        head_size = d_k // num_heads

        def split_heads(t):
            return t.reshape(B, S, num_heads, head_size).transpose(0, 2, 1, 3)
        q = split_heads(jnp.einsum('bsd,kd->bsk', x, q_proj_weight))
        k = split_heads(jnp.einsum('bsd,kd->bsk', x, k_proj_weight))
        v = split_heads(jnp.einsum('bsd,kd->bsk', x, v_proj_weight))
        scale = jnp.float32(head_size) ** (-0.5)
        scores = jnp.einsum('bhtc,bhkc->bhtk', q, k) * scale
        causal = jnp.tril(jnp.ones((S, S), dtype=bool))
        scores = jnp.where(causal, scores, -jnp.inf)
        attn = jax.nn.softmax(scores, axis=-1)
        out = jnp.einsum('bhtk,bhkc->bhtc', attn, v)
        out = out.transpose(0, 2, 1, 3).reshape(B, S, d_k)
        return jnp.einsum('bsv,dv->bsd', out, o_proj_weight)

    def _L0_ffn_ref(input, weight, bias):
        import jax, jax.numpy as jnp
        import numpy as np
        FP8_MAX = 448.0

        def quant_fp8(x):
            amax = jnp.max(jnp.abs(x)).astype(jnp.float32)
            scale = jnp.minimum(FP8_MAX / jnp.maximum(amax, 1e-12), FP8_MAX)
            x_fp8 = jnp.clip(x * scale, -FP8_MAX, FP8_MAX).astype(jnp.float8_e4m3fn)
            return (x_fp8, 1.0 / scale)
        prev_shape = input.shape
        x2d = input.reshape(-1, weight.shape[1])
        w_fp8, w_scale = quant_fp8(weight)
        x_fp8, x_scale = quant_fp8(x2d)
        acc = jnp.matmul(x_fp8.astype(jnp.float32), w_fp8.astype(jnp.float32).T)
        out2d = (acc * (x_scale * w_scale) + bias).astype(jnp.bfloat16)
        out = out2d.reshape(*prev_shape[:-1], weight.shape[0]).astype(input.dtype)
        return out
    x = L0_attn_x
    x = x + _L0_attn_ref(_layernorm(x, axis=-1), L0_attn_q_proj_weight, L0_attn_k_proj_weight, L0_attn_v_proj_weight, L0_attn_o_proj_weight)
    x = x + _L0_ffn_ref(_layernorm(x, axis=-1), L0_ffn_weight, L0_ffn_bias)
    return x

_drawn_inputs = setup_inputs


def setup_inputs(seed=0):
    import zlib

    import numpy as np

    out = dict(_drawn_inputs(seed))
    spreads = {}
    factors = {'L0_attn_q_proj_weight': 8.0,
     'L0_attn_k_proj_weight': 8.0,
     'L0_attn_v_proj_weight': 2.849,
     'L0_attn_o_proj_weight': 2.816,
     'L0_ffn_bias': 4.124}
    for name, (base, spread) in spreads.items():
        noise = np.random.default_rng([zlib.crc32(name.encode()), seed]).standard_normal(out[name].shape)
        drawn = base * np.exp(spread * noise) if base else spread * noise
        out[name] = jnp.asarray(drawn.astype(out[name].dtype))
    for name, factor in factors.items():
        out[name] = (out[name] * factor).astype(out[name].dtype)
    return out
```

```python
from contextlib import ExitStack

import concourse.bass as bass
from concourse import mybir

F32 = mybir.dt.float32
F32R = mybir.dt.float32r
BF16 = mybir.dt.bfloat16
U32 = mybir.dt.uint32
ALU = mybir.AluOpType
ACT = mybir.ActivationFunctionType
AX = mybir.AxisListType

B, S, D = 8, 1024, 512
HEADS = 16
HD = D // HEADS
P = 128
GH = P // HD
G = HEADS // GH
KC = D // P
QT = S // P
HALF = 512
TPH = HALF // P
TILES = B * QT
SCALE = HD ** -0.5
EPS = 1e-5
NEG = -3.0e38
MASKED = -1.0e30
KROWS = 3 * HD

STEPS = [(0, kt) for kt in range(TPH)] + [(1, kt) for kt in range(QT)]
NS = len(STEPS)
FIRST = (0, TPH)
LAST = (TPH - 1, NS - 1)


def first_column(s):
    qc, kt = STEPS[s]
    return max(0, kt - TPH * qc) * P


def on_diagonal(s):
    qc, kt = STEPS[s]
    return kt >= TPH * qc


RINGED = [s for s in range(NS) if s not in FIRST]
DIRECT = [s for s in range(NS) if STEPS[s][0] == 1 and on_diagonal(s)]
ADDED = [s for s in RINGED if s not in DIRECT]

MAX_UNITS = []
for half_of_q in range(2):
    for h in range(GH):
        for qt in range(half_of_q * TPH, (half_of_q + 1) * TPH):
            for kc in range(half_of_q + 1):
                last = kc == qt // TPH
                MAX_UNITS.append((h, qt, kc, (qt - TPH * kc + 1) * P if last else HALF, last))
NM = len(MAX_UNITS)

PROJECTIONS = [(0, 0), (1, 0), (0, 1), (1, 1), (2, 0), (2, 1)]
FILL = {0: "P0", 1: "P1", 2: "P2", 3: "P3 M4", 4: "M7", 5: "P4 M6", 6: "T0 M6", 7: "P5 M6",
        8: "T1 M6", 9: "M7", 10: "M6", 11: "C0"}
FILL_WITH_LN = {0: "P0", 1: "P1", 2: "P2", 3: "P3 M4", 4: "P4 M6", 5: "T0 P5 M5",
                6: "LA0 LA1 T1 M6 LB0", 7: "LA2 M6 LB1", 8: "LA3 M3 LB2 LA4 M3 LB3",
                9: "LA5 M7 LB4", 10: "LA6 M4 LB5 LA7 M4 LB6", 11: "C0 LB7"}


def fill_items(text, done):
    out = []
    for word in text.split():
        kind, n = word.rstrip("0123456789"), int(word.lstrip("PTMCLAB"))
        if kind == "M":
            out += [("M", done[0] + i) for i in range(n)]
            done[0] += n
        else:
            out.append((kind, n))
    return out


def batch_order(has_next):
    order = []
    for g in range(G):
        prepares = has_next or g < G - 1
        fill = (FILL_WITH_LN if g == G - 2 and has_next else FILL) if prepares else {}
        done = [0]
        for s in range(NS):
            items = fill_items(fill.get(s, ""), done)
            n = len(items)
            part = [items[n * k // 4:n * (k + 1) // 4] for k in range(4)]
            order += [("sc", g, (s, 0)), ("sc", g, (s, 1))]
            order += [(k, g, i) for k, i in part[0]]
            if s == 0 and g > 0:
                order += [("av", g - 1, NS - 1), ("avev", g - 1, 1)]
            if s > 0:
                order += [("av", g, s - 1)]
            if s - 1 == LAST[0]:
                order += [("avev", g, 0)]
            if s == 6:
                order += [("den0", g, 0)]
            order += [(k, g, i) for k, i in part[1]]
            order += [("sc", g, (s, 2))]
            order += [(k, g, i) for k, i in part[2]]
            order += [("sc", g, (s, 3))]
            order += [(k, g, i) for k, i in part[3]]
            if s == 7:
                order += [("norm", g, 0)]
            if s == 1 and g > 0:
                order += [("norm", g - 1, 1)]
        assert not fill or done[0] == NM
    order += [("av", G - 1, NS - 1), ("avev", G - 1, 1)]
    order += [("O", G - 1, 0), ("O", G - 1, 1), ("norm", G - 1, 1)]
    order += [("O", G - 1, tt) for tt in range(2, QT)] + [("stats", G - 1, 0)]
    return order


def first_order():
    order = [("LA", -1, 0), ("LA", -1, 1)]
    for i in range(QT):
        order += [("LB", -1, i)] + ([("LA", -1, i + 2)] if i + 2 < QT else [])
    order += [("P", -1, i) for i in range(4)] + [("P", -1, 4), ("T", -1, 0), ("P", -1, 5), ("T", -1, 1)]
    return order + [("M", -1, i) for i in range(NM)] + [("C", -1, 0)]


F_KINDS = ("P", "T", "C", "LB", "O")


def counted(order):
    f = high = bn = 0
    out = []
    for kind, g, i in order:
        out.append((kind, g, i, f, high, bn))
        f += kind in F_KINDS
        high += kind == "LB" or (kind == "P" and i < 4)
        bn += kind in ("LA", "O")
    return out, (f, high, bn)


FIRST_ITEMS, BEFORE = counted(first_order())
ITEMS, PER_BATCH = counted(batch_order(True))
LAST_ITEMS, _ = counted(batch_order(False))
LAST_LN = {place: next(f for kind, g, i, f, *_ in items if (kind, i) == ("LB", QT - 1))
           for place, items in ((-1, FIRST_ITEMS), (G - 1, ITEMS))}


def build_kernel(nc, x, wq, wk, wv, wo, ffn_w, ffn_b, out):
    x_t = x.rearrange("b (t p) d -> (b t) p d", p=P)
    out_t = out.rearrange("b (t p) d -> (b t) p d", p=P)
    w_scratch = nc.dram_tensor("w_scratch", (G, P, 6, KC, P), F32, kind="Internal").ap()
    x2_scratch = nc.dram_tensor("x2_scratch", (TILES, P, D), F32, kind="Internal").ap()

    ctx = ExitStack()
    with ctx:
        def sb(where, name, shape, dt=F32):
            return where.enter_context(nc.sbuf_tensor(name, shape, dt))

        def pb(where, name, shape, dt=F32):
            return where.enter_context(nc.psum_tensor(name, shape, dt))

        def sem(name):
            return ctx.enter_context(nc.semaphore(name))

        ident = sb(ctx, "ident", [P, P])
        ident_bf = sb(ctx, "ident_bf", [P, P], BF16)
        wo_T = sb(ctx, "wo_T", [P, KC, D])
        stats_all = sb(ctx, "stats_all", [P, TILES, 4])
        weights_block(nc, sb, pb, sem, (wq, wk, wv, wo), ident, ident_bf, wo_T, w_scratch)
        attention_block(nc, sb, pb, sem, x_t, x2_scratch, w_scratch, ident, ident_bf, wo_T, stats_all)
        linear_block(nc, sb, pb, sem, x2_scratch, ffn_w, ffn_b, out_t, ident_bf, stats_all)


def weights_block(nc, sb, pb, sem, weights, ident, ident_bf, wo_T, w_scratch):
    with ExitStack() as mem:
        w_rows = sb(mem, "w_rows", [P, 4, KC, D])
        w_high = sb(mem, "w_high", [P, 3, KC, D], F32R)
        w_low = sb(mem, "w_low", [P, 3, KC, D], F32R)
        bank = pb(mem, "w_bank", [P, 2, D])
        rows_in = [sem(f"w_rows_in{w}") for w in range(4)]
        zeroed, made = sem("w_zeroed"), sem("w_ident_made")
        turned, high_out, low_out = sem("w_turned"), sem("w_high_out"), sem("w_low_out")
        stored = sem("w_stored")
        units = [(w, c) for w in range(4) for c in range(KC)]

        with nc.Block() as block:
            @block.sync
            def _(sp):
                for w in range(4):
                    sp.dma_start(w_rows[:, w], weights[w].rearrange("(t p) d -> p t d", p=P)).then_inc(rows_in[w], 16)
                for w in range(3):
                    sp.wait_ge(low_out, KC * (w + 1))
                    for g in range(G):
                        for part, half in enumerate((w_high, w_low)):
                            sp.dma_start(w_scratch[g, :, 2 * w + part, :, :],
                                         half[:, w, :, g * P:(g + 1) * P].bitcast(F32)).then_inc(stored, 16)
                sp.wait_ge(stored, 16 * 3 * G * 2)

            @block.gpsimd
            def _(pool):
                nc.gpsimd.memset(ident[:], 0.0).then_inc(zeroed, 1)
                nc.gpsimd.memset(ident_bf[:], 0.0).then_inc(zeroed, 1)
                pool.wait_ge(zeroed, 2)
                for one in (ident, ident_bf):
                    nc.gpsimd.affine_select(out=one[:], in_=one[:], compare_op=ALU.not_equal, fill=1.0, base=0,
                                            pattern=[[-1, P]], channel_multiplier=1).then_inc(made, 1)

            @block.tensor
            def _(pe):
                pe.wait_ge(made, 2)
                for n, (w, c) in enumerate(units):
                    pe.wait_ge(rows_in[w], 16)
                    if n >= 2:
                        if n - 2 < 3 * KC:
                            pe.wait_ge(low_out, n - 1)
                        else:
                            pe.wait_ge(high_out, n - 1)
                    for t in range(KC):
                        last = nc.tensor.transpose(bank[:, n % 2, t * P:(t + 1) * P],
                                                   w_rows[:, w, t, c * P:(c + 1) * P], ident[:])
                    last.then_inc(turned, 1)

            @block.scalar
            def _(act):
                for n, (w, c) in enumerate(units):
                    act.wait_ge(turned, n + 1)
                    to = w_high[:, w, c] if w < 3 else wo_T[:, c]
                    nc.scalar.activation(to, bank[:, n % 2], ACT.Copy).then_inc(high_out, 1)

            @block.vector
            def _(dve):
                for n, (w, c) in enumerate(units[:3 * KC]):
                    dve.wait_ge(high_out, n + 1)
                    nc.vector.tensor_tensor(w_low[:, w, c], bank[:, n % 2], w_high[:, w, c].bitcast(F32),
                                            ALU.subtract).then_inc(low_out, 1)


def attention_block(nc, sb, pb, sem, x_t, x2_scratch, w_scratch, ident, ident_bf, wo_T, stats_all):
    with ExitStack() as mem:
        xT = [sb(mem, f"xT_{part}", [P, KC, S], F32R) for part in ("high", "low")]
        w_group = sb(mem, "w_group", [P, 6, KC, P], F32R)
        qk_part = sb(mem, "qk_part", [P, 2, 2, HALF], F32R)
        vT = sb(mem, "vT", [P, HALF])
        v_group = sb(mem, "v_group", [P, 2, QT, P])
        Qs = sb(mem, "Qs", [KROWS + 1, 2, GH, S], F32R)
        Ks = sb(mem, "Ks", [KROWS + 1, 2, GH, S], F32R)
        probs = sb(mem, "probs", [P, 2, GH, HALF])
        acc = sb(mem, "acc", [P, 2, GH, HALF])
        attn_T = sb(mem, "attn_T", [P, G, S])
        rec = sb(mem, "rec", [P, HALF])
        x_in = sb(mem, "x_in", [P, 2, D])
        x_norm = sb(mem, "x_norm", [P, 2, D])
        x_res = sb(mem, "x_res", [P, 4, D])
        ones = sb(mem, "ones", [P, HD])
        mask = sb(mem, "mask", [P, P])
        mask_T = sb(mem, "mask_T", [P, P], BF16)
        masked = sb(mem, "masked", [P, 2, P])
        maxima = sb(mem, "maxima", [P, 3, GH * QT])
        row_max = sb(mem, "row_max", [P, GH * QT])
        neg_max = sb(mem, "neg_max", [GH * QT, P], F32R)
        bn = sb(mem, "bn", [P, 2, 6])
        ln_stat = sb(mem, "ln_stat", [P, 2, 2])
        var_eps = sb(mem, "var_eps", [P, 1])
        rstd = sb(mem, "rstd", [P, 2])
        minus_half = sb(mem, "minus_half", [P, 1])
        x2_stat = sb(mem, "x2_stat", [P, QT, 4])

        score_bank = pb(mem, "score_bank", [P, 2, HALF])
        max_bank = pb(mem, "max_bank", [P, 2, HALF])
        fill_bank = pb(mem, "fill_bank", [P, 2, HALF])
        av_bank = pb(mem, "av_bank", [P, HALF])
        den_bank = pb(mem, "den_bank", [P, HALF])

        consts = sem("consts")
        ones_row = sem("ones_row")
        pool_passed, dve_passed, sp_passed = sem("pool_passed"), sem("dve_passed"), sem("sp_passed")
        scored = sem("scored")
        exp_done = sem("exp_done")
        added = sem("added")
        av_done = sem("av_done")
        den_done = sem("den_done")
        rec_done = sem("rec_done")
        av_out = sem("av_out")
        normed = sem("normed")
        max_full = sem("max_full")
        max_free = sem("max_free")
        row_ready = sem("row_ready")
        fill_full = sem("fill_full")
        fill_free = [sem(f"fill_free{i}") for i in range(2)]
        high_done = sem("high_done")
        vT_done = sem("vT_done")
        v_done = sem("v_done")
        stacked = [sem(f"stacked{i}") for i in range(2)]
        rows_in = sem("rows_in")
        w_in = sem("w_in")
        x_in_full = [sem(f"x_in_full{i}") for i in range(2)]
        bn_done = sem("bn_done")
        ln_stat_done = sem("ln_stat_done")
        eps_done = sem("eps_done")
        rstd_done = sem("rstd_done")
        x_norm_done = sem("x_norm_done")
        x_res_full = [sem(f"x_res_full{i}") for i in range(4)]
        x2_done = sem("x2_done")
        x2_stat_done = sem("x2_stat_done")
        stats_saved = sem("stats_saved")
        x2_stored = [sem(f"x2_stored{i}") for i in range(4)]

        UNIT_DMAS = 16 * 3 * GH

        def fill_no(b, f):
            if b is None:
                return f % 2, f // 2
            return (BEFORE[0] + f) % 2, b * (PER_BATCH[0] // 2) + (BEFORE[0] + f) // 2

        def fill_count(b, f):
            return f + 1 if b is None else b * PER_BATCH[0] + (BEFORE[0] + f + 1)

        def high_count(b, h):
            return h + 1 if b is None else b * PER_BATCH[1] + (BEFORE[1] + h + 1)

        def bn_count(b, n):
            return n + 1 if b is None else b * PER_BATCH[2] + (BEFORE[2] + n + 1)

        def per_group(b, g, each, more):
            return (0 if b is None else b * (each * G)) + (each * g + more)

        def after(b, g):
            return (0, 0) if b is None else (b, g + 1)

        def next_batch_tiles(b, i):
            return i if b is None else b * QT + (QT + i)

        def run(eng, body):
            body(None, FIRST_ITEMS)
            with eng.Fori(0, B - 1) as b:
                body(b, ITEMS)
            body(B - 1, LAST_ITEMS)

        with nc.Block() as block:
            @block.gpsimd
            def _(pool):
                nc.gpsimd.memset(ones[:], 1.0)
                nc.gpsimd.memset(minus_half[:], -0.5)
                nc.gpsimd.memset(maxima[:], NEG)
                nc.gpsimd.memset(mask_T[:], 0.0)
                nc.gpsimd.memset(mask[:], 0.0).then_inc(consts, 1)
                pool.wait_ge(consts, 1)
                nc.gpsimd.affine_select(out=mask[:], in_=mask[:], compare_op=ALU.is_ge, fill=MASKED, base=0,
                                        pattern=[[-1, P]], channel_multiplier=1).then_inc(consts, 1)
                nc.gpsimd.affine_select(out=mask_T[:], in_=mask_T[:], compare_op=ALU.is_ge, fill=MASKED, base=0,
                                        pattern=[[1, P]], channel_multiplier=-1).then_inc(consts, 1)

                def work(b, items):
                    for kind, g, i, f, high, bnn in items:
                        if kind == "LA":
                            n = next_batch_tiles(b, i)
                            if not (b is None and i == 0):
                                pool.wait_ge(rstd_done, n)
                            pool.wait_ge(ln_stat_done, n + 1)
                            pool.sem_inc(pool_passed, 1)
                            nc.gpsimd.tensor_scalar(var_eps[:], ln_stat[:, i % 2, 1:2], EPS, None,
                                                    ALU.add).then_inc(eps_done, 1)
                            pool.wait_ge(eps_done, n + 1)
                            pool.sem_inc(pool_passed, 1)
                            nc.gpsimd.tensor_tensor(rstd[:, i % 2:i % 2 + 1], var_eps[:], minus_half[:],
                                                    ALU.pow).then_inc(rstd_done, 1)
                        elif kind == "av" and i in ADDED:
                            qc = STEPS[i][0]
                            off = first_column(i)
                            pool.wait_ge(exp_done, per_group(b, g, GH * NS, GH * (i + 1) + 2))
                            pool.wait_ge(av_done, per_group(b, g, NS, FIRST[qc] + 1 + NS))
                            if ADDED.index(i) % (len(ADDED) // 2):
                                pool.wait_ge(added, per_group(b, g, len(ADDED), ADDED.index(i)))
                            for j in range(GH):
                                last = nc.gpsimd.tensor_tensor(acc[:, qc, j, off:], acc[:, qc, j, off:],
                                                               probs[:, RINGED.index(i) % 2, j, off:], ALU.add)
                            last.then_inc(added, 1)
                run(pool, work)

            @block.tensor
            def _(pe):
                pe.wait_ge(consts, 3)
                pe.wait_ge(ones_row, 1)

                def fill_target(b, f):
                    bank, before = fill_no(b, f)
                    pe.wait_ge(fill_free[bank], before + 1)
                    return bank

                def work(b, items):
                    for kind, g, i, f, high, bnn in items:
                        if kind == "P":
                            w, half = PROJECTIONS[i]
                            if i == 0:
                                pe.wait_ge(w_in, per_group(*after(b, g), 16, 16))
                                if g in (-1, G - 1):
                                    ln_bank, before = fill_no(b, LAST_LN[g])
                                    pe.wait_ge(fill_free[ln_bank], before + 2)
                            bank = fill_target(b, f)
                            cols = slice(half * HALF, (half + 1) * HALF)
                            for c in range(KC):
                                for wp, xp in ((0, 0), (1, 0), (0, 1)):
                                    last = nc.tensor.matmul(fill_bank[:, bank], w_group[:, 2 * w + wp, c],
                                                            xT[xp][:, c, cols], start=(c == 0 and wp + xp == 0),
                                                            stop=(c == KC - 1 and xp == 1))
                            last.then_inc(fill_full, 1)
                        elif kind == "T":
                            bank = fill_target(b, f)
                            pe.wait_ge(vT_done, per_group(*after(b, g), 2, i + 1))
                            for t in range(TPH):
                                last = nc.tensor.transpose(fill_bank[:, bank, t * P:(t + 1) * P],
                                                           vT[:, t * P:(t + 1) * P], ident[:])
                            last.then_inc(fill_full, 1)
                        elif kind == "M":
                            bn_, gn = after(b, g)
                            h, qt, kc, n, _ = MAX_UNITS[i]
                            if i == 0:
                                for slot in range(2):
                                    pe.wait_ge(stacked[slot], per_group(bn_, gn, 2 * UNIT_DMAS, UNIT_DMAS))
                            if i == GH * TPH:
                                for slot in range(2):
                                    pe.wait_ge(stacked[slot], per_group(bn_, gn, 2 * UNIT_DMAS, 2 * UNIT_DMAS))
                            pe.wait_ge(max_free, per_group(bn_, gn, NM, i + 1))
                            nc.tensor.matmul(max_bank[:, i % 2, 0:n],
                                             Qs[0:KROWS, gn % 2, h, qt * P:(qt + 1) * P],
                                             Ks[0:KROWS, gn % 2, h, kc * HALF:kc * HALF + n],
                                             start=True, stop=True).then_inc(max_full, 1)
                        elif kind == "C":
                            bank = fill_target(b, f)
                            pe.wait_ge(row_ready, per_group(*after(b, g), 1, 1))
                            nc.tensor.transpose(fill_bank[0:GH * QT, bank, 0:P], row_max[:],
                                                ident[:]).then_inc(fill_full, 1)
                        elif kind == "LB":
                            bank = fill_target(b, f)
                            pe.wait_ge(x_norm_done, next_batch_tiles(b, i) + 1)
                            for c in range(KC):
                                last = nc.tensor.transpose(fill_bank[:, bank, c * P:(c + 1) * P],
                                                           x_norm[:, i % 2, c * P:(c + 1) * P], ident[:])
                            last.then_inc(fill_full, 1)
                        elif kind == "O":
                            bank = fill_target(b, f)
                            pe.wait_ge(normed, b * (2 * G) + (2 * G + i // TPH))
                            for c in range(G):
                                last = nc.tensor.matmul(fill_bank[:, bank], attn_T[:, c, i * P:(i + 1) * P],
                                                        wo_T[:, c], start=(c == 0), stop=(c == G - 1))
                            last.then_inc(fill_full, 1)
                        elif kind == "sc":
                            s, j = i
                            qc, kt = STEPS[s]
                            off = first_column(s)
                            if s == 0 and j == 0:
                                pe.wait_ge(rows_in, per_group(b, g, 16 * GH, 16 * GH))
                                pe.wait_ge(v_done, per_group(b, g, 2, 2))
                            pe.wait_ge(exp_done, per_group(b, g, GH * NS, GH * s + j + 1))
                            q0 = qc * HALF
                            last = nc.tensor.matmul(score_bank[:, j % 2, off:], Ks[:, g % 2, j, kt * P:(kt + 1) * P],
                                                    Qs[:, g % 2, j, q0 + off:q0 + HALF],
                                                    start=True, stop=not on_diagonal(s))
                            if on_diagonal(s):
                                last = nc.tensor.matmul(score_bank[:, j % 2, off:off + P], ident_bf[:], mask_T[:],
                                                        start=False, stop=True)
                            last.then_inc(scored, 1)
                        elif kind == "av":
                            qc, kt = STEPS[i]
                            off = first_column(i)
                            half_no = per_group(b, g, 2, qc)
                            if i in FIRST:
                                pe.wait_ge(av_out, half_no + 1)
                            pe.wait_ge(exp_done, per_group(b, g, GH * NS, GH * (i + 1) + 2))
                            if i == DIRECT[0]:
                                pe.wait_ge(rec_done, half_no + 1)
                            for j in range(GH):
                                tile = acc[:, qc, j] if i in FIRST else probs[:, RINGED.index(i) % 2, j]
                                rows = slice(j * HD, (j + 1) * HD)
                                last = nc.tensor.matmul(av_bank[rows, off:], v_group[:, g % 2, kt, rows],
                                                        tile[:, off:], start=i in FIRST, stop=i in LAST)
                            if i in DIRECT:
                                if i == LAST[1]:
                                    pe.wait_ge(added, per_group(b, g, len(ADDED), len(ADDED)))
                                    for j in range(GH):
                                        nc.tensor.matmul(den_bank[j * HD:(j + 1) * HD, :], ones[:], acc[:, 1, j],
                                                         start=False, stop=False)
                                for j in range(GH):
                                    last = nc.tensor.matmul(den_bank[j * HD:(j + 1) * HD, off:], ones[:],
                                                            probs[:, RINGED.index(i) % 2, j, off:],
                                                            start=i == DIRECT[0], stop=i == LAST[1])
                            last.then_inc(av_done, 1)
                        elif kind == "den0":
                            half_no = per_group(b, g, 2, 0)
                            pe.wait_ge(rec_done, half_no + 1)
                            pe.wait_ge(added, per_group(b, g, len(ADDED), TPH - 1))
                            for j in range(GH):
                                last = nc.tensor.matmul(den_bank[j * HD:(j + 1) * HD, :], ones[:], acc[:, 0, j],
                                                        start=True, stop=True)
                            last.then_inc(den_done, 1)
                run(pe, work)

            @block.scalar
            def _(act):
                act.sem_inc(exp_done, 2)
                act.sem_inc(av_out, 1)

                def work(b, items):
                    for kind, g, i, f, high, bnn in items:
                        if kind in F_KINDS:
                            bank, before = fill_no(b, f)
                        if kind == "P":
                            act.wait_ge(fill_full, fill_count(b, f))
                            if i < 4:
                                bn_, gn = after(b, g)
                                if not (g < 0 and i < 2):
                                    act.wait_ge(stacked[i % 2], per_group(bn_, gn, 2 * UNIT_DMAS, i // 2 * UNIT_DMAS))
                                nc.scalar.activation(qk_part[:, i % 2, 0], fill_bank[:, bank],
                                                     ACT.Copy).then_inc(high_done, 1)
                            else:
                                nc.scalar.activation(vT[:], fill_bank[:, bank], ACT.Copy).then_inc(vT_done, 1)
                                act.wait_ge(vT_done, per_group(*after(b, g), 2, i - 4 + 1))
                                act.sem_inc(fill_free[bank], 1)
                        elif kind == "T":
                            act.wait_ge(fill_full, fill_count(b, f))
                            gn = after(b, g)[1]
                            nc.scalar.activation(v_group[:, gn % 2, i * TPH:(i + 1) * TPH],
                                                 fill_bank[:, bank].rearrange("p (t c) -> p t c", t=TPH),
                                                 ACT.Copy).then_inc(v_done, 1)
                            act.wait_ge(v_done, per_group(*after(b, g), 2, i + 1))
                            act.sem_inc(fill_free[bank], 1)
                        elif kind == "LB":
                            act.wait_ge(fill_full, fill_count(b, f))
                            nc.scalar.activation(xT[0][:, :, i * P:(i + 1) * P],
                                                 fill_bank[:, bank].rearrange("p (c t) -> p c t", c=KC),
                                                 ACT.Copy).then_inc(high_done, 1)
                        elif kind == "sc":
                            s, j = i
                            qc, kt = STEPS[s]
                            off = first_column(s)
                            if j == 0:
                                if s in FIRST:
                                    if qc == 0:
                                        act.wait_ge(den_done, per_group(b, g, 1, 1))
                                    else:
                                        act.wait_ge(av_done, per_group(b, g, NS, NS))
                                    tile_of = acc[:, qc]
                                else:
                                    k = RINGED.index(s)
                                    used = RINGED[k - 2] if k >= 2 else RINGED[k - 2] - NS
                                    act.wait_ge(av_done, per_group(b, g, NS, used + 1 + NS))
                                    if k >= 2 and used in ADDED:
                                        act.wait_ge(added, per_group(b, g, len(ADDED), ADDED.index(used) + 1))
                                    tile_of = probs[:, k % 2]
                            act.wait_ge(scored, per_group(b, g, GH * NS, GH * s + j + 1))
                            nc.scalar.activation(tile_of[:, j, off:], score_bank[:, j % 2, off:], ACT.Exp,
                                                 scale=SCALE).then_inc(exp_done, 1)
                        elif kind == "avev":
                            act.wait_ge(av_done, per_group(b, g, NS, LAST[i] + 1 + NS))
                            nc.scalar.activation(attn_T[:, g, i * HALF:(i + 1) * HALF], av_bank[:],
                                                 ACT.Copy).then_inc(av_out, 1)
                run(act, work)

            @block.vector
            def _(dve):
                dve.sem_inc(max_free, 2)
                dve.sem_inc(rec_done, 1)
                dve.sem_inc(normed, 1)
                dve.sem_inc(stats_saved, 1)
                dve.sem_inc(fill_free[0], 1)
                dve.sem_inc(fill_free[1], 1)
                nc.vector.memset(Ks[KROWS:KROWS + 1].bitcast(F32), 1.0).then_inc(ones_row, 1)
                dve.wait_ge(consts, 2)

                def low_part(b, item):
                    kind, g, i, f, high, bnn = item
                    bank, before = fill_no(b, f)
                    if kind == "P":
                        dve.wait_ge(high_done, high_count(b, high))
                        nc.vector.tensor_tensor(qk_part[:, i % 2, 1], fill_bank[:, bank],
                                                qk_part[:, i % 2, 0].bitcast(F32),
                                                ALU.subtract).then_inc(fill_free[bank], 1)
                    elif kind == "LB":
                        dve.wait_ge(high_done, high_count(b, high))
                        cols = slice(i * P, (i + 1) * P)
                        nc.vector.tensor_tensor(xT[1][:, :, cols],
                                                fill_bank[:, bank].rearrange("p (c t) -> p c t", c=KC),
                                                xT[0][:, :, cols].bitcast(F32),
                                                ALU.subtract).then_inc(fill_free[bank], 1)
                    elif kind == "C":
                        dve.wait_ge(fill_full, fill_count(b, f))
                        nc.vector.tensor_scalar(neg_max[:], fill_bank[0:GH * QT, bank, 0:P], -1.0, None,
                                                ALU.mult).then_inc(fill_free[bank], 1)

                def work(b, items):
                    waiting = []
                    for item in items:
                        kind, g, i, f, high, bnn = item
                        if waiting and (kind in F_KINDS or kind == "sc"):
                            low_part(b, waiting.pop())
                        if kind == "LA":
                            n = next_batch_tiles(b, i)
                            dve.wait_ge(x_in_full[i % 2], (0 if b is None else (b + 1) * (8 * QT)) + 16 * (i // 2 + 1))
                            if not (b is None and i < 2):
                                dve.wait_ge(x_norm_done, n - 1)
                            nc.vector.bn_stats(bn[:, i % 2], x_in[:, i % 2]).then_inc(bn_done, 1)
                            dve.wait_ge(bn_done, bn_count(b, bnn))
                            dve.sem_inc(dve_passed, 1)
                            nc.vector.bn_aggr(ln_stat[:, i % 2], bn[:, i % 2]).then_inc(ln_stat_done, 1)
                        elif kind == "LB":
                            n = next_batch_tiles(b, i)
                            dve.wait_ge(rstd_done, n + 1)
                            nc.vector.tensor_scalar(x_norm[:, i % 2], x_in[:, i % 2], ln_stat[:, i % 2, 0:1],
                                                    rstd[:, i % 2:i % 2 + 1], ALU.subtract,
                                                    ALU.mult).then_inc(x_norm_done, 1)
                            waiting.append(item)
                        elif kind == "P" and i < 4:
                            waiting.append(item)
                        elif kind == "M":
                            bn_, gn = after(b, g)
                            h, qt, kc, n, last = MAX_UNITS[i]
                            full = n - P if last else n
                            col = h * QT + qt
                            if last:
                                dve.wait_ge(max_free, per_group(bn_, gn, NM, i - 1 + 2))
                            dve.wait_ge(max_full, per_group(bn_, gn, NM, i + 1))
                            if full:
                                ins = nc.vector.tensor_reduce(maxima[:, kc, col:col + 1], max_bank[:, i % 2, 0:full],
                                                              AX.X, ALU.max)
                            elif last:
                                dve.sem_inc(dve_passed, 1)
                            if last:
                                ins = nc.vector.tensor_tensor_reduce(
                                    out=masked[:, i % 2], in0=max_bank[:, i % 2, full:n], in1=mask[:], scale=1.0, scalar=NEG,
                                    op0=ALU.add, op1=ALU.max, accum_out=maxima[:, 2, col:col + 1])
                            ins.then_inc(max_free, 1)
                        elif kind == "C":
                            dve.wait_ge(max_free, per_group(*after(b, g), NM, NM + 2))
                            nc.vector.tensor_reduce(row_max[:], maxima[:].rearrange("p a n -> p n a"), AX.X,
                                                    ALU.max).then_inc(row_ready, 1)
                            waiting.append(item)
                        elif kind == "norm":
                            if i == 0:
                                dve.wait_ge(den_done, per_group(b, g, 1, 2))
                            else:
                                dve.wait_ge(av_done, per_group(b, g, NS, NS + NS))
                            dve.wait_ge(normed, per_group(b, g, 2, i + 1))
                            nc.vector.reciprocal(rec[:], den_bank[:]).then_inc(rec_done, 1)
                            dve.wait_ge(rec_done, per_group(b, g, 2, i + 2))
                            dve.wait_ge(av_out, per_group(b, g, 2, i + 2))
                            part = attn_T[:, g, i * HALF:(i + 1) * HALF]
                            nc.vector.tensor_tensor(part, part, rec[:], ALU.mult).then_inc(normed, 1)
                        elif kind == "O":
                            bank, before = fill_no(b, f)
                            x2 = x_res[:, i % 4]
                            if i == 0:
                                dve.wait_ge(stats_saved, b + 1)
                            if i >= 2:
                                dve.wait_ge(x2_stat_done, b * QT + (i - 1))
                            dve.wait_ge(x_res_full[i % 4], b * 32 + 16 * (i // 4 + 1))
                            dve.wait_ge(fill_full, fill_count(b, f))
                            nc.vector.tensor_tensor(x2, fill_bank[:, bank], x2, ALU.add).then_inc(x2_done, 1)
                            dve.wait_ge(x2_done, b * QT + (i + 1))
                            dve.sem_inc(fill_free[bank], 1)
                            nc.vector.bn_stats(bn[:, i % 2], x2).then_inc(bn_done, 1)
                            nc.vector.tensor_reduce(x2_stat[:, i, 2:3], x2, AX.X, ALU.max)
                            nc.vector.tensor_reduce(x2_stat[:, i, 3:4], x2, AX.X, ALU.min)
                            dve.wait_ge(bn_done, bn_count(b, bnn))
                            dve.sem_inc(dve_passed, 1)
                            nc.vector.bn_aggr(x2_stat[:, i, 0:2], bn[:, i % 2]).then_inc(x2_stat_done, 1)
                        elif kind == "stats":
                            dve.wait_ge(x2_stat_done, b * QT + QT)
                            nc.vector.tensor_copy(stats_all[:, bass.ds(b * QT, QT), :],
                                                  x2_stat[:]).then_inc(stats_saved, 1)
                    if waiting:
                        low_part(b, waiting.pop())

                dve.sem_inc(den_done, 1)
                dve.sem_inc(av_done, NS)
                run(dve, work)

            @block.sync
            def _(sp):
                def load_x(b, i):
                    sp.sem_inc(sp_passed, 1)
                    sp.dma_start(x_in[:, i % 2], x_t[bass.ds(next_batch_tiles(b, i), 1)].rearrange(
                        "o p d -> p (o d)")).then_inc(x_in_full[i % 2], 16)

                for k in range(4):
                    sp.sem_inc(x2_stored[k], 1)

                def load_residual(b, i):
                    sp.sem_inc(sp_passed, 1)
                    sp.dma_start(x_res[:, i % 4], x_t[bass.ds(b * QT + i, 1)].rearrange(
                        "o p d -> p (o d)")).then_inc(x_res_full[i % 4], 16)

                def work(b, items):
                    if b is None:
                        sp.dma_start(w_group[:].bitcast(F32), w_scratch[0]).then_inc(w_in, 16)
                        load_x(b, 0)
                        load_x(b, 1)
                    for kind, g, i, f, high, bnn in items:
                        if kind in F_KINDS:
                            bank, before = fill_no(b, f)
                        if kind == "P" and i < 4:
                            gn = after(b, g)[1]
                            w, half = PROJECTIONS[i]
                            if g >= 0 and i == 0:
                                sp.wait_ge(scored, per_group(b, g, GH * NS, 1))
                            sp.wait_ge(fill_free[bank], before + 2)
                            stack = (Qs, Ks)[w]
                            parts = ((0, 1, 0), (0, 0, 1))[w]
                            for n, part in enumerate(parts):
                                for h in range(GH):
                                    sp.dma_start(stack[n * HD:(n + 1) * HD, gn % 2, h,
                                                       half * HALF:(half + 1) * HALF].bitcast(F32),
                                                 qk_part[h * HD:(h + 1) * HD, i % 2, part].bitcast(F32)
                                                 ).then_inc(stacked[i % 2], 16)
                        elif kind == "P" and i == 5:
                            sp.wait_ge(fill_full, fill_count(b, f))
                            if b is None or not (isinstance(b, int) and b == B - 1 and g == G - 2):
                                sp.dma_start(w_group[:].bitcast(F32), w_scratch[(g + 2) % G]).then_inc(w_in, 16)
                        elif kind == "C":
                            gn = after(b, g)[1]
                            sp.wait_ge(fill_free[bank], before + 2)
                            for h in range(GH):
                                sp.dma_start(
                                    Qs[KROWS:KROWS + 1, gn % 2, h, :].bitcast(F32).rearrange("p (t q) -> p t q", t=QT),
                                    neg_max[h * QT:(h + 1) * QT, :].bitcast(F32)).then_inc(rows_in, 16)
                        elif kind == "LB" and i + 2 < QT:
                            sp.wait_ge(x_norm_done, next_batch_tiles(b, i) + 1)
                            load_x(b, i + 2)
                        elif kind == "sc" and g == G - 2 and i == (0, 0) and items is ITEMS:
                            sp.wait_ge(x_norm_done, b * QT + QT)
                            load_x(b, 0)
                            load_x(b, 1)
                        elif kind == "sc" and g == G - 1 and i == (0, 0):
                            for k in range(4):
                                sp.wait_ge(x2_stored[k], b * 32 + 1)
                                sp.sem_inc(sp_passed, 1)
                            sp.wait_ge(stats_saved, b + 1)
                            for k in range(4):
                                load_residual(b, k)
                        elif kind == "O":
                            sp.wait_ge(x2_done, b * QT + (i + 1))
                            sp.sem_inc(sp_passed, 1)
                            sp.dma_start(x2_scratch[bass.ds(b * QT + i, 1)].rearrange("o p d -> p (o d)"),
                                         x_res[:, i % 4]).then_inc(x2_stored[i % 4], 16)
                            if 1 <= i <= 4:
                                sp.wait_ge(x2_stored[i - 1], b * 32 + 17)
                                sp.sem_inc(sp_passed, 1)
                                sp.wait_ge(x2_stat_done, b * QT + i)
                                load_residual(b, i + 3)
                run(sp, work)
                for k in range(4):
                    sp.wait_ge(x2_stored[k], 32 * B + 1)


def linear_block(nc, sb, pb, sem, x2_scratch, ffn_w, ffn_b, out_t, ident_bf, stats_all):
    UT = 2
    UNITS = TILES // UT
    SLOTS = 4
    FP8_MAX = 448.0
    SMALLEST = 2.0 ** -6
    MAGIC = 1.5 * 2.0 ** 20
    EXPONENT = 0x7F800000
    RMAX = bass.bass_isa.ReduceOp.max
    with ExitStack() as mem:
        w_rows = sb(mem, "f_rows", [P, KC, D])
        w_power = sb(mem, "f_power_w", [P, KC, D])
        w_q = sb(mem, "f_q", [P, KC, D], BF16)
        w_T = sb(mem, "f_wT", [P, KC, D], BF16)
        bias = sb(mem, "f_bias", [P, D])
        dev = sb(mem, "f_dev", [P, 3, TILES])
        minus_half = sb(mem, "f_minus_half", [P, TILES])
        rstd = sb(mem, "f_rstd", [P, TILES])
        mul_col = sb(mem, "f_mul", [P, TILES])
        add_col = sb(mem, "f_add", [P, TILES])
        parts = sb(mem, "f_parts", [P, 4])
        amax = sb(mem, "f_amax", [P, 2])
        scale = sb(mem, "f_scale", [P, 2])
        inverse = sb(mem, "f_inverse", [P, 2])
        back = sb(mem, "f_back", [P, 1])
        x2 = sb(mem, "f_x2", [P, SLOTS, UT, D])
        z = sb(mem, "f_z", [P, 2, UT, D])
        power = sb(mem, "f_power", [P, 2, UT, D])
        zq = sb(mem, "f_zq", [P, 2, UT, D], BF16)
        zT = sb(mem, "f_zT", [P, UT, KC, P], BF16)
        y = sb(mem, "f_y", [P, 2, UT, D], BF16)
        t_bank = pb(mem, "f_t_bank", [P, UT, 2 * HALF], BF16)
        o_bank = pb(mem, "f_o_bank", [P, 2 * UT, D])

        w_in, b_in = sem("f_w_in"), sem("f_b_in")
        small = sem("f_small")
        const, eps_out, rstd_out, all_max = sem("f_const"), sem("f_eps"), sem("f_rstd"), sem("f_all_max")
        w_turned, w_out = sem("f_w_turned"), sem("f_w_out")
        x2_in = [sem(f"f_x2_in{k}") for k in range(SLOTS)]
        z_done = sem("f_z_done")
        p_done = sem("f_p_done")
        r_done = sem("f_r_done")
        q_done = sem("f_q_done")
        t_full, t_out = sem("f_t_full"), sem("f_t_out")
        o_full, o_out = sem("f_o_full"), sem("f_o_out")
        y_done = sem("f_y_done")
        stored = [sem(f"f_stored{k}") for k in range(SLOTS)]
        sp_passed = sem("f_sp_passed")

        def run(eng, step, lag):
            for k in range(SLOTS):
                step(0, k)
            with eng.Fori(1, UNITS // SLOTS) as i:
                for k in range(SLOTS):
                    step(i, k)
            for k in range(lag):
                step(UNITS // SLOTS, k)

        def number(i, k):
            n = i * SLOTS + k
            return None if isinstance(n, int) and not 0 <= n < UNITS else n

        with nc.Block() as block:
            @block.sync
            def _(sp):
                sp.dma_start(w_rows[:], ffn_w.rearrange("(t p) d -> p t d", p=P)).then_inc(w_in, 16)
                sp.dma_start(bias[:], ffn_b.rearrange("(o n) -> o n", o=1).broadcast_to((P, D))).then_inc(b_in, 16)

                def load(i, k):
                    sp.sem_inc(sp_passed, 1)
                    sp.dma_start(x2[:, k % SLOTS],
                                 x2_scratch[bass.ds((i * SLOTS + k) * UT, UT)].rearrange("t p d -> p t d")
                                 ).then_inc(x2_in[k % SLOTS], 16)

                def step(i, k):
                    if not (isinstance(i, int) and i == UNITS // SLOTS - 1 and k >= 2):
                        if not (isinstance(i, int) and i == 0 and k < 2):
                            sp.wait_ge(stored[(k + 2) % SLOTS], i * 16 + 16 * (k // 2))
                        load(i, k + 2)
                    sp.wait_ge(y_done, i * SLOTS + (k + 1))
                    sp.sem_inc(sp_passed, 1)
                    sp.dma_start(out_t[bass.ds((i * SLOTS + k) * UT, UT)].rearrange("t p d -> p t d"),
                                 x2[:, k]).then_inc(stored[k], 16)
                load(0, 0)
                load(0, 1)
                for k in range(SLOTS):
                    step(0, k)
                with sp.Fori(1, UNITS // SLOTS - 1) as i:
                    for k in range(SLOTS):
                        step(i, k)
                for k in range(SLOTS):
                    step(UNITS // SLOTS - 1, k)
                for k in range(SLOTS):
                    sp.wait_ge(stored[k], 16 * UNITS // SLOTS)

            @block.gpsimd
            def _(pool):
                nc.gpsimd.memset(minus_half[:], -0.5)
                nc.gpsimd.tensor_scalar(rstd[:], stats_all[:, :, 1], EPS, None, ALU.add).then_inc(eps_out, 1)
                pool.wait_ge(eps_out, 1)
                nc.gpsimd.tensor_tensor(rstd[:], rstd[:], minus_half[:], ALU.pow).then_inc(rstd_out, 1)
                pool.wait_ge(small, 8)
                nc.gpsimd.partition_all_reduce(amax[:], parts[:, 0:2], P, RMAX).then_inc(all_max, 1)

                def step(i, k):
                    u = number(i, k)
                    if u is not None:
                        pool.wait_ge(p_done, u * 3 + 3)
                        if not (isinstance(u, int) and u < 2):
                            pool.wait_ge(t_full, u * UT - UT)
                        nc.gpsimd.tensor_tensor(zq[:, k % 2], z[:, k % 2], power[:, k % 2],
                                                ALU.subtract).then_inc(r_done, 1)
                    u = number(i, k - 2)
                    if u is not None:
                        pool.wait_ge(o_out, u * UT + UT)
                        slot = x2[:, (k - 2) % SLOTS]
                        nc.gpsimd.tensor_tensor(slot, slot, y[:, k % 2], ALU.add).then_inc(y_done, 1)
                run(pool, step, 2)

            @block.vector
            def _(dve):
                done = [0]

                def chained(ins):
                    done[0] += 1
                    ins.then_inc(small, 1)
                    dve.wait_ge(small, done[0])

                mean, largest, least = stats_all[:, :, 0], stats_all[:, :, 2], stats_all[:, :, 3]
                nc.vector.tensor_tensor(dev[:, 0], largest, mean, ALU.subtract)
                chained(nc.vector.tensor_tensor(dev[:, 1], mean, least, ALU.subtract))
                chained(nc.vector.tensor_tensor(dev[:, 0], dev[:, 0], dev[:, 1], ALU.max))
                dve.wait_ge(rstd_out, 1)
                chained(nc.vector.tensor_tensor(dev[:, 0], dev[:, 0], rstd[:], ALU.mult))
                chained(nc.vector.tensor_reduce(parts[:, 0:1], dev[:, 0], AX.X, ALU.max))
                dve.wait_ge(w_in, 16)
                all_w = w_rows[:].rearrange("p t d -> p (t d)")
                chained(nc.vector.tensor_reduce(parts[:, 2:3], all_w, AX.X, ALU.max))
                chained(nc.vector.tensor_reduce(parts[:, 3:4], all_w, AX.X, ALU.min))
                chained(nc.vector.tensor_scalar(parts[:, 3:4], parts[:, 3:4], -1.0, None, ALU.mult))
                chained(nc.vector.tensor_tensor(parts[:, 1:2], parts[:, 2:3], parts[:, 3:4], ALU.max))
                dve.wait_ge(all_max, 1)
                chained(nc.vector.tensor_scalar(amax[:], amax[:], 1e-12, None, ALU.max))
                chained(nc.vector.reciprocal(scale[:], amax[:]))
                chained(nc.vector.tensor_scalar(scale[:], scale[:], FP8_MAX, FP8_MAX, ALU.mult, ALU.min))
                chained(nc.vector.reciprocal(inverse[:], scale[:]))
                chained(nc.vector.tensor_tensor(back[:], inverse[:, 0:1], inverse[:, 1:2], ALU.mult))
                chained(nc.vector.tensor_scalar(mul_col[:], rstd[:], scale[:, 0:1], None, ALU.mult))
                chained(nc.vector.scalar_tensor_tensor(out=add_col[:], in0=mean, scalar=-1.0, in1=mul_col[:],
                                                       op0=ALU.mult, op1=ALU.mult))
                chained(nc.vector.tensor_scalar(all_w, all_w, scale[:, 1:2], None, ALU.mult))
                all_p = w_power[:].rearrange("p t d -> p (t d)")
                chained(nc.vector.tensor_scalar(all_p.bitcast(U32), all_w.bitcast(U32), EXPONENT, None,
                                                ALU.bitwise_and))
                chained(nc.vector.tensor_scalar(all_p, all_p, SMALLEST, MAGIC, ALU.max, ALU.mult))
                chained(nc.vector.tensor_tensor(all_w, all_w, all_p, ALU.add))
                chained(nc.vector.tensor_tensor(all_w, all_w, all_p, ALU.subtract))
                chained(nc.vector.tensor_scalar(w_q[:].rearrange("p t d -> p (t d)"), all_w, FP8_MAX, -FP8_MAX,
                                                ALU.min, ALU.max))
                dve.wait_ge(b_in, 16)

                def step(i, k):
                    u = number(i, k)
                    if u is not None:
                        zk = z[:, k % 2].rearrange("p t d -> p (t d)")
                        pk = power[:, k % 2].rearrange("p t d -> p (t d)")
                        dve.wait_ge(z_done, u + 1)
                        nc.vector.tensor_scalar(pk.bitcast(U32), zk.bitcast(U32), EXPONENT, None,
                                                ALU.bitwise_and).then_inc(p_done, 1)
                        dve.wait_ge(p_done, u * 3 + 1)
                        nc.vector.tensor_scalar(pk, pk, SMALLEST, MAGIC, ALU.max, ALU.mult).then_inc(p_done, 1)
                        dve.wait_ge(p_done, u * 3 + 2)
                        nc.vector.tensor_tensor(zk, zk, pk, ALU.add).then_inc(p_done, 1)
                    u = number(i, k - 1)
                    if u is not None:
                        dve.wait_ge(r_done, u + 1)
                        rounded = zq[:, (k - 1) % 2].rearrange("p t d -> p (t d)")
                        nc.vector.tensor_scalar(rounded, rounded, FP8_MAX, -FP8_MAX, ALU.min,
                                                ALU.max).then_inc(q_done, 1)
                    u = number(i, k - 2)
                    if u is not None:
                        if not (isinstance(u, int) and u < 2):
                            dve.wait_ge(y_done, u - 1)
                        for t in range(UT):
                            dve.wait_ge(o_full, u * UT + (t + 1))
                            nc.vector.scalar_tensor_tensor(out=y[:, k % 2, t], in0=o_bank[:, k % 2 * UT + t],
                                                           scalar=back[:], in1=bias[:], op0=ALU.mult,
                                                           op1=ALU.add).then_inc(o_out, 1)
                run(dve, step, 2)

            @block.tensor
            def _(pe):
                for c in range(KC):
                    if c == 0:
                        pe.wait_ge(small, 21)
                    if c >= UT:
                        pe.wait_ge(w_out, c - UT + 1)
                    for t in range(KC):
                        last = nc.tensor.transpose(t_bank[:, c % UT, t * P:(t + 1) * P],
                                                   w_q[:, t, c * P:(c + 1) * P], ident_bf[:])
                    last.then_inc(w_turned, 1)
                pe.wait_ge(w_out, KC)

                def step(i, k):
                    u = number(i, k - 1)
                    if u is None:
                        return
                    for t in range(UT):
                        if t == 0:
                            pe.wait_ge(q_done, u + 1)
                        if not (isinstance(u, int) and u < 1):
                            pe.wait_ge(t_out, u * UT + (t + 1 - UT))
                        for c in range(KC):
                            last = nc.tensor.transpose(t_bank[:, t, c * P:(c + 1) * P],
                                                       zq[:, (k - 1) % 2, t, c * P:(c + 1) * P], ident_bf[:])
                        last.then_inc(t_full, 1)
                    for t in range(UT):
                        pe.wait_ge(t_out, u * UT + (t + 1))
                        if not (isinstance(u, int) and u < 2):
                            pe.wait_ge(o_out, u * UT + (t + 1 - 2 * UT))
                        for c in range(KC):
                            last = nc.tensor.matmul(o_bank[:, (k - 1) % 2 * UT + t], zT[:, t, c], w_T[:, c],
                                                    start=c == 0, stop=c == KC - 1)
                        last.then_inc(o_full, 1)
                run(pe, step, 1)

            @block.scalar
            def _(act):
                for c in range(KC):
                    act.wait_ge(w_turned, c + 1)
                    nc.scalar.activation(w_T[:, c], t_bank[:, c % UT, 0:D], ACT.Copy).then_inc(w_out, 1)

                def step(i, k):
                    u = number(i, k)
                    if u is not None:
                        act.wait_ge(x2_in[k], i * 16 + 16)
                        if not (isinstance(u, int) and u < 2):
                            act.wait_ge(r_done, u - 1)
                        for t in range(UT):
                            col = bass.ds(u * UT + t, 1)
                            last = nc.scalar.activation(z[:, k % 2, t], x2[:, k, t], ACT.Identity,
                                                        bias=add_col[:, col], scale=mul_col[:, col])
                        last.then_inc(z_done, 1)
                    u = number(i, k - 1)
                    if u is not None:
                        for t in range(UT):
                            act.wait_ge(t_full, u * UT + (t + 1))
                            if not (isinstance(u, int) and u < 1):
                                act.wait_ge(o_full, u * UT + (t + 1 - UT))
                            nc.scalar.activation(zT[:, t].rearrange("p c t -> p (c t)"), t_bank[:, t, 0:D],
                                                 ACT.Copy).then_inc(t_out, 1)
                act.wait_ge(small, 14)
                run(act, step, 1)


_INS = ["L0_attn_x", "L0_attn_q_proj_weight", "L0_attn_k_proj_weight", "L0_attn_v_proj_weight",
        "L0_attn_o_proj_weight", "L0_ffn_weight", "L0_ffn_bias"]


def kernel(**inputs):
    import numpy as _np
    import concourse.bacc as _bacc
    from concourse.bass_utils import run_bass_kernel_spmd as _run

    nc = _bacc.Bacc("TRN2", target_bir_lowering=False, num_devices=1)
    arrays, args = {}, []
    for name in _INS:
        a = _np.ascontiguousarray(inputs[name])
        arrays[f"in_{name}"] = a
        args.append(nc.dram_tensor(f"in_{name}", a.shape, mybir.dt.from_np(a.dtype), kind="ExternalInput").ap())
    out = nc.dram_tensor("out_x", (B, S, D), F32, kind="ExternalOutput").ap()
    nc.disable_value_cache = True
    build_kernel(nc, *args, out)
    r = _run(nc, [arrays], core_ids=[0])
    return r.results[0]["out_x"]
```

```python
from contextlib import ExitStack

import concourse.bass as bass
from concourse import mybir

F32 = mybir.dt.float32
F32R = mybir.dt.float32r
BF16 = mybir.dt.bfloat16
U32 = mybir.dt.uint32
ALU = mybir.AluOpType
ACT = mybir.ActivationFunctionType
AX = mybir.AxisListType

B, S, D = 8, 1024, 512
HEADS = 16
HD = D // HEADS
P = 128
GH = P // HD
G = HEADS // GH
KC = D // P
QT = S // P
HALF = 512
TPH = HALF // P
TILES = B * QT
SCALE = HD ** -0.5
EPS = 1e-5
NEG = -3.0e38
MASKED = -1.0e30
KROWS = 3 * HD

FP8_MAX = 448.0
SMALLEST = 2.0 ** -6
MAGIC = 1.5 * 2.0 ** 20
EXPONENT = 0x7F800000
RMAX = bass.bass_isa.ReduceOp.max
FW_STEPS = 14

STEPS = [(0, kt) for kt in range(TPH)] + [(1, kt) for kt in range(QT)]
NS = len(STEPS)
FIRST = (0, TPH)
LAST = (TPH - 1, NS - 1)


def first_column(s):
    qc, kt = STEPS[s]
    return max(0, kt - TPH * qc) * P


def on_diagonal(s):
    qc, kt = STEPS[s]
    return kt >= TPH * qc


RINGED = [s for s in range(NS) if s not in FIRST]
DIRECT = [s for s in range(NS) if STEPS[s][0] == 1 and on_diagonal(s)]
ADDED = [s for s in RINGED if s not in DIRECT]

MAX_UNITS = []
for half_of_q in range(2):
    for h in range(GH):
        for qt in range(half_of_q * TPH, (half_of_q + 1) * TPH):
            for kc in range(half_of_q + 1):
                last = kc == qt // TPH
                MAX_UNITS.append((h, qt, kc, (qt - TPH * kc + 1) * P if last else HALF, last))
NM = len(MAX_UNITS)
HALF_UNITS = GH * TPH

PROJECTIONS = [(0, 0), (1, 0), (0, 1), (1, 1), (2, 0), (2, 1)]
QUARTERS = 4
PIECES = KC


def spread(items, start, end):
    return [(start + (end - start) * (n + 0.5) / len(items), item) for n, item in enumerate(items)]


def projection(u, ahead=1):
    return [("P", (u, piece, ahead)) for piece in range(PIECES)]


AT = {"heads": (0.0, 0.25, 0.55, 0.8), "av": 0.4, "step": 60, "row": 0.028, "qk1": 0.13, "v": (0.22, 0.4),
      "early": (0.66, 0.795), "max": ((0.0, 0.3), (0.34, 0.88)), "late_qk0": 0.15, "late_qk1": 0.306,
      "late_max": ((0.26, 0.42), (0.44, 0.9)), "late_v": (0.34, 0.47), "ln_v": (0.221, 0.35),
      "norm": (0.02, 0.5), "last_norm": (0.93, 1.0), "ln": 0.49, "ln_step": 0.056}


def group_order(g, has_next):
    placed = []
    with_stats = has_next and g == G - 3
    with_ln = has_next and g == G - 2
    late_start = g == G - 1
    starts_after_next = g != G - 2
    length = [HALF + AT["step"] - first_column(s) for s in range(NS)]
    at = [sum(length[:s]) / sum(length) for s in range(NS + 1)]
    for s in range(NS):
        for j, share in enumerate(AT["heads"]):
            placed.append((at[s] + share * (at[s + 1] - at[s]), ("sc", g, (s, j))))
        late = at[s] + AT["av"] * (at[s + 1] - at[s])
        if s > 0:
            placed.append((late, ("av", g, s - 1)))
        elif g > 0:
            placed += [(late, ("av", g - 1, NS - 1)), (late + 1e-4, ("out", g - 1, 1)),
                       (late + 2e-4, ("dout", g - 1, 1))]
        if s - 1 == LAST[0]:
            placed.append((late + 1e-4, ("out", g, 0)))
    placed += [(at[6] + 1e-3, ("den", g, 0)), (at[6] + 1.1e-3, ("dout", g, 0))]
    if g > 0:
        placed += spread([("norm", g - 1, i) for i in range(2 * QUARTERS)], *AT["norm"])
    if g == G - 1:
        placed += spread([("norm", g, i) for i in range(QUARTERS)], *AT["last_norm"])
    more = []
    if with_stats:
        more += spread([("LS", i) for i in range(QT)], 0.05, 0.90)
    if has_next or g < G - 1:
        if late_start:
            more += spread(projection(0) + projection(1), 0.0, AT["late_qk0"])
            more += spread(projection(2) + projection(3), AT["late_qk0"], AT["late_qk1"])
        else:
            more += spread(projection(2) + projection(3), 0.0, AT["qk1"])
        v0, v1 = AT["ln_v" if with_ln else "late_v" if late_start else "v"]
        more += spread(projection(4), v0, v0 + 0.08) + [(v0 + 0.12, ("T", 0))]
        more += spread(projection(5), v1, v1 + 0.08) + [(v1 + 0.12, ("T", 1))]
        if with_ln:
            more.append((0.1, ("LR", 0)))
            for i in range(QT):
                place = AT["ln"] + AT["ln_step"] * i
                more += [(place, ("LA", i)), (place + 0.75 * AT["ln_step"], ("LB", i))]
        elif starts_after_next:
            more += spread(projection(0, 2) + projection(1, 2), *AT["early"])
        for units, (start, end) in zip((range(HALF_UNITS), range(HALF_UNITS, NM)),
                                       AT["late_max" if late_start else "max"]):
            cost = [MAX_UNITS[i][3] + 70 for i in units]
            for n, i in enumerate(units):
                more.append((start + (end - start) * sum(cost[:n]) / sum(cost), ("M", i)))
        more.append((end + AT["row"], ("C", 0)))
    placed += [(place, (kind, g, i)) for place, (kind, i) in more]
    return [item for _, item in sorted(placed, key=lambda x: x[0])]


def batch_order(has_next):
    order = []
    for g in range(G):
        order += group_order(g, has_next)
    order += [("av", G - 1, NS - 1), ("out", G - 1, 1), ("dout", G - 1, 1)]
    order += [("O", G - 1, 0)] + [("norm", G - 1, i) for i in range(QUARTERS, 2 * QUARTERS)]
    order += [("O", G - 1, tt) for tt in range(1, QT)] + [("stats", G - 1, 0)]
    return order


def first_order():
    order = [("LS", -1, i) for i in range(QT)] + [("LR", -1, 0), ("LA", -1, 0)]
    for i in range(QT):
        order += ([("LA", -1, i + 1)] if i + 1 < QT else []) + [("LB", -1, i)]
    for u in range(4):
        order += [("P", -1, i) for _, i in projection(u)]
    more = [("M", i) for i in range(NM)]
    others = projection(4) + [("T", 0)] + projection(5) + [("T", 1)] + projection(0, 2) + projection(1, 2)
    merged = sorted(spread(more, 0, 1) + spread(others, 0, 0.8), key=lambda x: x[0])
    return order + [(kind, -1, i) for _, (kind, i) in merged] + [("C", -1, 0)]


F_KINDS = ("P", "T", "C", "LB", "O")


def is_last_piece(kind, i):
    return kind != "P" or i[1] == PIECES - 1


def counted(order):
    f = high = bn = 0
    out = []
    open_unit = False
    for kind, g, i in order:
        assert not (open_unit and kind in F_KINDS and kind != "P")
        out.append((kind, g, i, f, high, bn))
        if kind == "P":
            open_unit = not is_last_piece(kind, i)
        if is_last_piece(kind, i):
            f += kind in F_KINDS
            high += kind == "LB" or (kind == "P" and i[0] < 4)
            bn += kind in ("LS", "O")
    return out, (f, high, bn)


FIRST_ITEMS, BEFORE = counted(first_order())
ITEMS, PER_BATCH = counted(batch_order(True))
LAST_ITEMS, _ = counted(batch_order(False))
LAST_LN = {place: next(f for kind, g, i, f, *_ in items if (kind, i) == ("LB", QT - 1))
           for place, items in ((-1, FIRST_ITEMS), (G - 1, ITEMS))}


def build_kernel(nc, x, wq, wk, wv, wo, ffn_w, ffn_b, out):
    x_t = x.rearrange("b (t p) d -> (b t) p d", p=P)
    out_t = out.rearrange("b (t p) d -> (b t) p d", p=P)
    w_scratch = nc.dram_tensor("w_scratch", (G, P, 6, KC, P), F32, kind="Internal").ap()
    x2_scratch = nc.dram_tensor("x2_scratch", (TILES, P, D), F32, kind="Internal").ap()
    fw_scratch = nc.dram_tensor("fw_scratch", (P, KC, D), BF16, kind="Internal").ap()
    qk_scratch = nc.dram_tensor("qk_scratch", (4, 2, P, HALF), F32, kind="Internal").ap()

    ctx = ExitStack()
    with ctx:
        def sb(where, name, shape, dt=F32):
            return where.enter_context(nc.sbuf_tensor(name, shape, dt))

        def pb(where, name, shape, dt=F32):
            return where.enter_context(nc.psum_tensor(name, shape, dt))

        def sem(name):
            return ctx.enter_context(nc.semaphore(name))

        ident = sb(ctx, "ident", [P, P])
        ident_bf = sb(ctx, "ident_bf", [P, P], BF16)
        wo_T = sb(ctx, "wo_T", [P, KC, D])
        stats_all = sb(ctx, "stats_all", [P, TILES, 4])
        fw_inverse = sb(ctx, "fw_inverse", [P, 1])
        weights_block(nc, sb, pb, sem, (wq, wk, wv, wo), ffn_w, ident, ident_bf, wo_T, w_scratch, fw_scratch,
                      fw_inverse)
        attention_block(nc, sb, pb, sem, x_t, x2_scratch, w_scratch, qk_scratch, ident, ident_bf, wo_T, stats_all)
        linear_block(nc, sb, pb, sem, x2_scratch, fw_scratch, fw_inverse, ffn_b, out_t, ident_bf, stats_all)


def weights_block(nc, sb, pb, sem, weights, ffn_w, ident, ident_bf, wo_T, w_scratch, fw_scratch, fw_inverse):
    with ExitStack() as mem:
        fw = sb(mem, "fw", [P, KC, D])
        fw_power = sb(mem, "fw_power", [P, KC, D])
        fw_q = sb(mem, "fw_q", [P, KC, D], BF16)
        fw_T = sb(mem, "fw_T", [P, KC, D], BF16)
        fw_max = sb(mem, "fw_max", [P, 4])
        fw_scale = sb(mem, "fw_scale", [P, 1])
        fw_bank = pb(mem, "fw_bank", [P, 2, 2 * D], BF16)
        fw_in, fw_step, fw_all_max = sem("fw_in"), sem("fw_step"), sem("fw_all_max")
        fw_turned, fw_out, fw_stored = sem("fw_turned"), sem("fw_out"), sem("fw_stored")
        w_rows = sb(mem, "w_rows", [P, 4, KC, D])
        w_high = sb(mem, "w_high", [P, 3, KC, D], F32R)
        w_low = sb(mem, "w_low", [P, 3, KC, D], F32R)
        bank = pb(mem, "w_bank", [P, 2, D])
        rows_in = [sem(f"w_rows_in{w}") for w in range(4)]
        zeroed, made = sem("w_zeroed"), sem("w_ident_made")
        turned, high_out, low_out = sem("w_turned"), sem("w_high_out"), sem("w_low_out")
        stored = sem("w_stored")
        units = [(w, c) for w in range(4) for c in range(KC)]

        with nc.Block() as block:
            @block.sync
            def _(sp):
                for w in range(4):
                    sp.dma_start(w_rows[:, w], weights[w].rearrange("(t p) d -> p t d", p=P)).then_inc(rows_in[w], 16)
                    if w == 1:
                        sp.dma_start(fw[:], ffn_w.rearrange("(t p) d -> p t d", p=P)).then_inc(fw_in, 16)
                for w in range(3):
                    sp.wait_ge(low_out, KC * (w + 1))
                    for g in range(G):
                        for part, half in enumerate((w_high, w_low)):
                            sp.dma_start(w_scratch[g, :, 2 * w + part, :, :],
                                         half[:, w, :, g * P:(g + 1) * P].bitcast(F32)).then_inc(stored, 16)
                sp.wait_ge(fw_out, KC)
                sp.dma_start(fw_scratch[:], fw_T[:]).then_inc(fw_stored, 16)
                sp.wait_ge(stored, 16 * 3 * G * 2)
                sp.wait_ge(fw_stored, 16)

            @block.gpsimd
            def _(pool):
                nc.gpsimd.memset(ident[:], 0.0).then_inc(zeroed, 1)
                nc.gpsimd.memset(ident_bf[:], 0.0).then_inc(zeroed, 1)
                pool.wait_ge(zeroed, 2)
                for one in (ident, ident_bf):
                    nc.gpsimd.affine_select(out=one[:], in_=one[:], compare_op=ALU.not_equal, fill=1.0, base=0,
                                            pattern=[[-1, P]], channel_multiplier=1).then_inc(made, 1)
                pool.wait_ge(fw_step, 4)
                nc.gpsimd.partition_all_reduce(fw_max[:, 3:4], fw_max[:, 2:3], P, RMAX).then_inc(fw_all_max, 1)

            @block.tensor
            def _(pe):
                pe.wait_ge(made, 2)
                for n, (w, c) in enumerate(units):
                    pe.wait_ge(rows_in[w], 16)
                    if n >= 2:
                        if n - 2 < 3 * KC:
                            pe.wait_ge(low_out, n - 1)
                        else:
                            pe.wait_ge(high_out, n - 1)
                    for t in range(KC):
                        last = nc.tensor.transpose(bank[:, n % 2, t * P:(t + 1) * P],
                                                   w_rows[:, w, t, c * P:(c + 1) * P], ident[:])
                    last.then_inc(turned, 1)
                pe.wait_ge(fw_step, FW_STEPS)
                for c in range(KC):
                    if c >= 2:
                        pe.wait_ge(fw_out, c - 1)
                    for t in range(KC):
                        last = nc.tensor.transpose(fw_bank[:, c % 2, t * P:(t + 1) * P],
                                                   fw_q[:, t, c * P:(c + 1) * P], ident_bf[:])
                    last.then_inc(fw_turned, 1)

            @block.scalar
            def _(act):
                for n, (w, c) in enumerate(units):
                    act.wait_ge(turned, n + 1)
                    to = w_high[:, w, c] if w < 3 else wo_T[:, c]
                    nc.scalar.activation(to, bank[:, n % 2], ACT.Copy).then_inc(high_out, 1)
                for c in range(KC):
                    act.wait_ge(fw_turned, c + 1)
                    nc.scalar.activation(fw_T[:, c], fw_bank[:, c % 2, 0:D], ACT.Copy).then_inc(fw_out, 1)

            @block.vector
            def _(dve):
                done = [0]

                def chained(ins):
                    done[0] += 1
                    ins.then_inc(fw_step, 1)
                    dve.wait_ge(fw_step, done[0])

                all_w = fw[:].rearrange("p t d -> p (t d)")
                all_p = fw_power[:].rearrange("p t d -> p (t d)")
                for n, (w, c) in enumerate(units[:3 * KC]):
                    dve.wait_ge(high_out, n + 1)
                    nc.vector.tensor_tensor(w_low[:, w, c], bank[:, n % 2], w_high[:, w, c].bitcast(F32),
                                            ALU.subtract).then_inc(low_out, 1)
                    if n == 4:
                        dve.wait_ge(fw_in, 16)
                        chained(nc.vector.tensor_reduce(fw_max[:, 0:1], all_w, AX.X, ALU.max))
                    elif n == 5:
                        chained(nc.vector.tensor_reduce(fw_max[:, 1:2], all_w, AX.X, ALU.min))
                        chained(nc.vector.tensor_scalar(fw_max[:, 1:2], fw_max[:, 1:2], -1.0, None, ALU.mult))
                        chained(nc.vector.tensor_tensor(fw_max[:, 2:3], fw_max[:, 0:1], fw_max[:, 1:2], ALU.max))
                    elif n == 6:
                        dve.wait_ge(fw_all_max, 1)
                        chained(nc.vector.tensor_scalar(fw_max[:, 3:4], fw_max[:, 3:4], 1e-12, None, ALU.max))
                        chained(nc.vector.reciprocal(fw_scale[:], fw_max[:, 3:4]))
                        chained(nc.vector.tensor_scalar(fw_scale[:], fw_scale[:], FP8_MAX, FP8_MAX, ALU.mult,
                                                        ALU.min))
                        chained(nc.vector.reciprocal(fw_inverse[:], fw_scale[:]))
                        chained(nc.vector.tensor_scalar(all_w, all_w, fw_scale[:], None, ALU.mult))
                    elif n == 7:
                        chained(nc.vector.tensor_scalar(all_p.bitcast(U32), all_w.bitcast(U32), EXPONENT, None,
                                                        ALU.bitwise_and))
                    elif n == 8:
                        chained(nc.vector.tensor_scalar(all_p, all_p, SMALLEST, MAGIC, ALU.max, ALU.mult))
                    elif n == 9:
                        chained(nc.vector.tensor_tensor(all_w, all_w, all_p, ALU.add))
                    elif n == 10:
                        chained(nc.vector.tensor_tensor(all_w, all_w, all_p, ALU.subtract))
                    elif n == 11:
                        chained(nc.vector.tensor_scalar(fw_q[:].rearrange("p t d -> p (t d)"), all_w, FP8_MAX,
                                                        -FP8_MAX, ALU.min, ALU.max))
                assert done[0] == FW_STEPS


def attention_block(nc, sb, pb, sem, x_t, x2_scratch, w_scratch, qk_scratch, ident, ident_bf, wo_T, stats_all):
    with ExitStack() as mem:
        xT = [sb(mem, f"xT_{part}", [P, KC, S], F32R) for part in ("high", "low")]
        w_group = sb(mem, "w_group", [P, 6, KC, P], F32R)
        qk_part = sb(mem, "qk_part", [P, 2, 2, HALF], F32R)
        vT = sb(mem, "vT", [P, HALF])
        v_group = sb(mem, "v_group", [P, 2, QT, P])
        Qs = sb(mem, "Qs", [KROWS + 1, 2, GH, S], F32R)
        Ks = sb(mem, "Ks", [KROWS + 1, 2, GH, S], F32R)
        probs = sb(mem, "probs", [P, 2, GH, HALF])
        acc = sb(mem, "acc", [P, 2, GH, HALF])
        attn_T = sb(mem, "attn_T", [P, G, S])
        den = sb(mem, "den", [P, 2, HALF])
        x_in = sb(mem, "x_in", [P, 2, D])
        x_norm = sb(mem, "x_norm", [P, 2, D])
        x_res = sb(mem, "x_res", [P, 4, D])
        ones = sb(mem, "ones", [P, HD])
        mask = sb(mem, "mask", [P, P], BF16)
        mask_T = sb(mem, "mask_T", [P, P], BF16)
        maxima = sb(mem, "maxima", [P, 2, GH * QT])
        row_max = sb(mem, "row_max", [P, GH * QT])
        neg_max = sb(mem, "neg_max", [GH * QT, P], F32R)
        bn = sb(mem, "bn", [P, 2, 6])
        ln_stat = sb(mem, "ln_stat", [P, QT, 2])
        var_eps = sb(mem, "var_eps", [P, QT])
        rstd = sb(mem, "rstd", [P, QT])
        minus_half = sb(mem, "minus_half", [P, QT])
        x2_stat = sb(mem, "x2_stat", [P, QT, 4])

        score_bank = pb(mem, "score_bank", [P, 2, HALF])
        max_bank = pb(mem, "max_bank", [P, 2, HALF])
        fill_bank = pb(mem, "fill_bank", [P, 2, HALF])
        av_bank = pb(mem, "av_bank", [P, HALF])
        den_bank = pb(mem, "den_bank", [P, HALF])

        consts = sem("consts")
        ones_row = sem("ones_row")
        pool_passed, dve_passed, sp_passed = sem("pool_passed"), sem("dve_passed"), sem("sp_passed")
        scored = sem("scored")
        exp_done = sem("exp_done")
        added = sem("added")
        av_done = sem("av_done")
        den_done = sem("den_done")
        den_out = sem("den_out")
        rec_done = sem("rec_done")
        av_out = sem("av_out")
        normed = sem("normed")
        max_full = sem("max_full")
        max_free = sem("max_free")
        row_ready = sem("row_ready")
        fill_full = sem("fill_full")
        fill_free = [sem(f"fill_free{i}") for i in range(2)]
        high_done = sem("high_done")
        vT_done = sem("vT_done")
        v_done = sem("v_done")
        parked = [sem(f"parked{i}") for i in range(2)]
        stacked = [sem(f"stacked{i}") for i in range(2)]
        rows_in = sem("rows_in")
        w_qk_in, w_v_in = sem("w_qk_in"), sem("w_v_in")
        x_first_in = [sem(f"x_first_in{i}") for i in range(2)]
        x_in_full = [sem(f"x_in_full{i}") for i in range(2)]
        bn_done = sem("bn_done")
        ln_stat_done = sem("ln_stat_done")
        eps_done = sem("eps_done")
        rstd_done = sem("rstd_done")
        x_norm_done = sem("x_norm_done")
        x_res_full = [sem(f"x_res_full{i}") for i in range(4)]
        x2_done = sem("x2_done")
        x2_stat_done = sem("x2_stat_done")
        stats_saved = sem("stats_saved")
        x2_stored = [sem(f"x2_stored{i}") for i in range(4)]

        UNIT_DMAS = 16 * 3

        def fill_no(b, f):
            if b is None:
                return f % 2, f // 2
            return (BEFORE[0] + f) % 2, b * (PER_BATCH[0] // 2) + (BEFORE[0] + f) // 2

        def fill_count(b, f):
            return f + 1 if b is None else b * PER_BATCH[0] + (BEFORE[0] + f + 1)

        def high_count(b, h):
            return h + 1 if b is None else b * PER_BATCH[1] + (BEFORE[1] + h + 1)

        def bn_count(b, n):
            return n + 1 if b is None else b * PER_BATCH[2] + (BEFORE[2] + n + 1)

        def per_group(b, g, each, more):
            return (0 if b is None else b * (each * G)) + (each * g + more)

        def after(b, g, ahead=1):
            return (0, ahead - 1) if b is None else (b, g + ahead)

        def next_batch_tiles(b, i):
            return i if b is None else b * QT + (QT + i)

        def token_tile(b, i):
            return probs[:, i // GH, i % GH] if b is None else x_in[:, i % 2]

        def wait_token_tile(eng, b, n):
            if b is None:
                eng.wait_ge(x_first_in[n % QT // GH], 16)
            else:
                eng.wait_ge(x_in_full[n % 2], b * (16 * QT) + 16 * (n // 2 + 1))

        def run(eng, body):
            body(None, FIRST_ITEMS)
            with eng.Fori(0, B - 1) as b:
                body(b, ITEMS)
            body(B - 1, LAST_ITEMS)

        with nc.Block() as block:
            @block.gpsimd
            def _(pool):
                nc.gpsimd.memset(ones[:], 1.0)
                nc.gpsimd.memset(minus_half[:], -0.5)
                nc.gpsimd.memset(maxima[:], NEG)
                nc.gpsimd.memset(mask_T[:], 0.0)
                nc.gpsimd.memset(mask[:], 0.0).then_inc(consts, 1)
                pool.wait_ge(consts, 1)
                nc.gpsimd.affine_select(out=mask[:], in_=mask[:], compare_op=ALU.is_ge, fill=MASKED, base=0,
                                        pattern=[[-1, P]], channel_multiplier=1).then_inc(consts, 1)
                nc.gpsimd.affine_select(out=mask_T[:], in_=mask_T[:], compare_op=ALU.is_ge, fill=MASKED, base=0,
                                        pattern=[[1, P]], channel_multiplier=-1).then_inc(consts, 1)
                pool.wait_ge(consts, 3)
                nc.gpsimd.memset(Ks[KROWS:KROWS + 1].bitcast(F32), 1.0).then_inc(ones_row, 1)
                pool.wait_ge(ones_row, 1)

                def work(b, items):
                    for kind, g, i, f, high, bnn in items:
                        if kind == "LR":
                            n = next_batch_tiles(b, 0)
                            if b is not None:
                                pool.wait_ge(rstd_done, b + 1)
                                pool.wait_ge(x_norm_done, n)
                            pool.wait_ge(ln_stat_done, n + QT)
                            pool.sem_inc(pool_passed, 1)
                            nc.gpsimd.tensor_scalar(var_eps[:], ln_stat[:, :, 1], EPS, None,
                                                    ALU.add).then_inc(eps_done, 1)
                            pool.wait_ge(eps_done, 1 if b is None else b + 2)
                            pool.sem_inc(pool_passed, 1)
                            nc.gpsimd.tensor_tensor(rstd[:], var_eps[:], minus_half[:],
                                                    ALU.pow).then_inc(rstd_done, 1)
                        elif kind == "av" and i in ADDED:
                            qc = STEPS[i][0]
                            off = first_column(i)
                            pool.wait_ge(exp_done, per_group(b, g, GH * NS, GH * (i + 1) + 2))
                            pool.wait_ge(av_done, per_group(b, g, NS, FIRST[qc] + 1 + NS))
                            if ADDED.index(i) % (len(ADDED) // 2):
                                pool.wait_ge(added, per_group(b, g, len(ADDED), ADDED.index(i)))
                            for j in range(GH):
                                last = nc.gpsimd.tensor_tensor(acc[:, qc, j, off:], acc[:, qc, j, off:],
                                                               probs[:, RINGED.index(i) % 2, j, off:], ALU.add)
                            last.then_inc(added, 1)
                        elif kind == "norm" and i % QUARTERS == QUARTERS - 1:
                            half = i // QUARTERS
                            pool.wait_ge(rec_done, per_group(b, g, 2 * QUARTERS, i + 1))
                            pool.wait_ge(av_out, per_group(b, g, 2, half + 2))
                            part = attn_T[:, g, half * HALF:(half + 1) * HALF]
                            nc.gpsimd.tensor_tensor(part, part, den[:, half], ALU.mult).then_inc(normed, 1)
                run(pool, work)

            @block.tensor
            def _(pe):
                pe.wait_ge(consts, 3)

                def fill_target(b, f):
                    bank, before = fill_no(b, f)
                    pe.wait_ge(fill_free[bank], before + 1)
                    return bank

                def work(b, items):
                    for kind, g, i, f, high, bnn in items:
                        if kind == "P":
                            unit, c, ahead = i
                            w, half = PROJECTIONS[unit]
                            if unit == 0 and c == 0:
                                pe.wait_ge(w_qk_in, per_group(*after(b, g, ahead), 16, 16))
                            if unit == 4 and c == 0:
                                pe.wait_ge(w_v_in, per_group(*after(b, g, ahead), 16, 16))
                            if i == (0, 0, 1):
                                if g in (-1, G - 1):
                                    ln_bank, before = fill_no(b, LAST_LN[g])
                                    pe.wait_ge(fill_free[ln_bank], before + 2)
                            bank = fill_target(b, f) if c == 0 else fill_no(b, f)[0]
                            cols = slice(half * HALF, (half + 1) * HALF)
                            for wp, xp in ((0, 0), (1, 0), (0, 1)):
                                last = nc.tensor.matmul(fill_bank[:, bank], w_group[:, 2 * w + wp, c],
                                                        xT[xp][:, c, cols], start=(c == 0 and wp + xp == 0),
                                                        stop=(c == KC - 1 and xp == 1))
                            if is_last_piece(kind, i):
                                last.then_inc(fill_full, 1)
                        elif kind == "T":
                            bank = fill_target(b, f)
                            pe.wait_ge(vT_done, per_group(*after(b, g), 2, i + 1))
                            for t in range(TPH):
                                last = nc.tensor.transpose(fill_bank[:, bank, t * P:(t + 1) * P],
                                                           vT[:, t * P:(t + 1) * P], ident[:])
                            last.then_inc(fill_full, 1)
                        elif kind == "M":
                            bn_, gn = after(b, g)
                            h, qt, kc, n, diagonal = MAX_UNITS[i]
                            if i == 0:
                                for slot in range(2):
                                    pe.wait_ge(stacked[slot], per_group(bn_, gn, 2 * UNIT_DMAS, UNIT_DMAS))
                            if i == GH * TPH:
                                for slot in range(2):
                                    pe.wait_ge(stacked[slot], per_group(bn_, gn, 2 * UNIT_DMAS, 2 * UNIT_DMAS))
                            pe.wait_ge(max_free, per_group(bn_, gn, NM, i + 1))
                            last = nc.tensor.matmul(max_bank[:, i % 2, 0:n],
                                                    Qs[0:KROWS, gn % 2, h, qt * P:(qt + 1) * P],
                                                    Ks[0:KROWS, gn % 2, h, kc * HALF:kc * HALF + n],
                                                    start=True, stop=not diagonal)
                            if diagonal:
                                last = nc.tensor.matmul(max_bank[:, i % 2, n - P:n], ident_bf[:], mask[:],
                                                        start=False, stop=True)
                            last.then_inc(max_full, 1)
                        elif kind == "C":
                            bank = fill_target(b, f)
                            pe.wait_ge(row_ready, per_group(*after(b, g), 1, 1))
                            nc.tensor.transpose(fill_bank[0:GH * QT, bank, 0:P], row_max[:],
                                                ident[:]).then_inc(fill_full, 1)
                        elif kind == "LB":
                            bank = fill_target(b, f)
                            pe.wait_ge(x_norm_done, next_batch_tiles(b, i) + 1)
                            for c in range(KC):
                                last = nc.tensor.transpose(fill_bank[:, bank, c * P:(c + 1) * P],
                                                           x_norm[:, i % 2, c * P:(c + 1) * P], ident[:])
                            last.then_inc(fill_full, 1)
                        elif kind == "O":
                            bank = fill_target(b, f)
                            pe.wait_ge(normed, b * (2 * G) + (2 * G + 1 + i // TPH))
                            for c in range(G):
                                last = nc.tensor.matmul(fill_bank[:, bank], attn_T[:, c, i * P:(i + 1) * P],
                                                        wo_T[:, c], start=(c == 0), stop=(c == G - 1))
                            last.then_inc(fill_full, 1)
                        elif kind == "sc":
                            s, j = i
                            qc, kt = STEPS[s]
                            off = first_column(s)
                            if b is not None and s == 0 and j == 0 and g == 0:
                                pe.wait_ge(ones_row, 1)
                            if s == 0 and j == 0:
                                pe.wait_ge(rows_in, per_group(b, g, 16 * GH, 16 * GH))
                                pe.wait_ge(v_done, per_group(b, g, 2, 2))
                            pe.wait_ge(exp_done, per_group(b, g, GH * NS, GH * s + j + 1))
                            q0 = qc * HALF
                            last = nc.tensor.matmul(score_bank[:, j % 2, off:], Ks[:, g % 2, j, kt * P:(kt + 1) * P],
                                                    Qs[:, g % 2, j, q0 + off:q0 + HALF],
                                                    start=True, stop=not on_diagonal(s))
                            if on_diagonal(s):
                                last = nc.tensor.matmul(score_bank[:, j % 2, off:off + P], ident_bf[:], mask_T[:],
                                                        start=False, stop=True)
                            last.then_inc(scored, 1)
                        elif kind == "av":
                            qc, kt = STEPS[i]
                            off = first_column(i)
                            half_no = per_group(b, g, 2, qc)
                            if i in FIRST:
                                pe.wait_ge(av_out, half_no + 1)
                            pe.wait_ge(exp_done, per_group(b, g, GH * NS, GH * (i + 1) + 2))
                            if i == DIRECT[0]:
                                pe.wait_ge(den_out, half_no + 1)
                            for j in range(GH):
                                tile = acc[:, qc, j] if i in FIRST else probs[:, RINGED.index(i) % 2, j]
                                rows = slice(j * HD, (j + 1) * HD)
                                last = nc.tensor.matmul(av_bank[rows, off:], v_group[:, g % 2, kt, rows],
                                                        tile[:, off:], start=i in FIRST, stop=i in LAST)
                            if i in DIRECT:
                                if i == LAST[1]:
                                    pe.wait_ge(added, per_group(b, g, len(ADDED), len(ADDED)))
                                    for j in range(GH):
                                        nc.tensor.matmul(den_bank[j * HD:(j + 1) * HD, :], ones[:], acc[:, 1, j],
                                                         start=False, stop=False)
                                for j in range(GH):
                                    last = nc.tensor.matmul(den_bank[j * HD:(j + 1) * HD, off:], ones[:],
                                                            probs[:, RINGED.index(i) % 2, j, off:],
                                                            start=i == DIRECT[0], stop=i == LAST[1])
                            last.then_inc(av_done, 1)
                        elif kind == "den":
                            pe.wait_ge(den_out, per_group(b, g, 2, 1))
                            pe.wait_ge(added, per_group(b, g, len(ADDED), TPH - 1))
                            for j in range(GH):
                                last = nc.tensor.matmul(den_bank[j * HD:(j + 1) * HD, :], ones[:], acc[:, 0, j],
                                                        start=True, stop=True)
                            last.then_inc(den_done, 1)
                run(pe, work)

            @block.scalar
            def _(act):
                act.sem_inc(exp_done, 2)
                act.sem_inc(av_out, 1)
                act.sem_inc(den_out, 1)

                def work(b, items):
                    for kind, g, i, f, high, bnn in items:
                        if kind in F_KINDS:
                            bank, before = fill_no(b, f)
                        if kind == "P" and is_last_piece(kind, i):
                            act.wait_ge(fill_full, fill_count(b, f))
                            unit, _, ahead = i
                            bn_, gn = after(b, g, ahead)
                            if unit < 4:
                                if not (g < 0 and unit < 2 and ahead == 1):
                                    act.wait_ge(parked[unit % 2], per_group(bn_, gn, 2 * 16, unit // 2 * 16))
                                nc.scalar.activation(qk_part[:, unit % 2, 0], fill_bank[:, bank],
                                                     ACT.Copy).then_inc(high_done, 1)
                            else:
                                nc.scalar.activation(vT[:], fill_bank[:, bank], ACT.Copy).then_inc(vT_done, 1)
                                act.wait_ge(vT_done, per_group(bn_, gn, 2, unit - 4 + 1))
                                act.sem_inc(fill_free[bank], 1)
                        elif kind == "T":
                            act.wait_ge(fill_full, fill_count(b, f))
                            gn = after(b, g)[1]
                            nc.scalar.activation(v_group[:, gn % 2, i * TPH:(i + 1) * TPH],
                                                 fill_bank[:, bank].rearrange("p (t c) -> p t c", t=TPH),
                                                 ACT.Copy).then_inc(v_done, 1)
                            act.wait_ge(v_done, per_group(*after(b, g), 2, i + 1))
                            act.sem_inc(fill_free[bank], 1)
                        elif kind == "LB":
                            act.wait_ge(fill_full, fill_count(b, f))
                            nc.scalar.activation(xT[0][:, :, i * P:(i + 1) * P],
                                                 fill_bank[:, bank].rearrange("p (c t) -> p c t", c=KC),
                                                 ACT.Copy).then_inc(high_done, 1)
                        elif kind == "sc":
                            s, j = i
                            qc, kt = STEPS[s]
                            off = first_column(s)
                            if j == 0:
                                if s in FIRST:
                                    if qc == 0:
                                        act.wait_ge(den_done, per_group(b, g, 1, 1))
                                    else:
                                        act.wait_ge(av_done, per_group(b, g, NS, NS))
                                    tile_of = acc[:, qc]
                                else:
                                    k = RINGED.index(s)
                                    used = RINGED[k - 2] if k >= 2 else RINGED[k - 2] - NS
                                    act.wait_ge(av_done, per_group(b, g, NS, used + 1 + NS))
                                    if k >= 2 and used in ADDED:
                                        act.wait_ge(added, per_group(b, g, len(ADDED), ADDED.index(used) + 1))
                                    tile_of = probs[:, k % 2]
                            act.wait_ge(scored, per_group(b, g, GH * NS, GH * s + j + 1))
                            nc.scalar.activation(tile_of[:, j, off:], score_bank[:, j % 2, off:], ACT.Exp,
                                                 scale=SCALE).then_inc(exp_done, 1)
                        elif kind == "dout":
                            if i == 0:
                                act.wait_ge(den_done, per_group(b, g, 1, 2))
                            else:
                                act.wait_ge(av_done, per_group(b, g, NS, NS + NS))
                            act.wait_ge(normed, per_group(b, g, 2, i + 1))
                            nc.scalar.activation(den[:, i], den_bank[:], ACT.Copy).then_inc(den_out, 1)
                        elif kind == "out":
                            act.wait_ge(av_done, per_group(b, g, NS, LAST[i] + 1 + NS))
                            nc.scalar.activation(attn_T[:, g, i * HALF:(i + 1) * HALF], av_bank[:],
                                                 ACT.Copy).then_inc(av_out, 1)
                run(act, work)

            @block.vector
            def _(dve):
                dve.sem_inc(max_free, 2)
                dve.sem_inc(normed, 2)
                dve.sem_inc(stats_saved, 1)
                dve.sem_inc(fill_free[0], 1)
                dve.sem_inc(fill_free[1], 1)
                dve.wait_ge(consts, 2)

                def low_part(b, item):
                    kind, g, i, f, high, bnn = item
                    bank, before = fill_no(b, f)
                    if kind == "P":
                        slot = i[0] % 2
                        dve.wait_ge(high_done, high_count(b, high))
                        nc.vector.tensor_tensor(qk_part[:, slot, 1], fill_bank[:, bank],
                                                qk_part[:, slot, 0].bitcast(F32),
                                                ALU.subtract).then_inc(fill_free[bank], 1)
                    elif kind == "LB":
                        dve.wait_ge(high_done, high_count(b, high))
                        cols = slice(i * P, (i + 1) * P)
                        nc.vector.tensor_tensor(xT[1][:, :, cols],
                                                fill_bank[:, bank].rearrange("p (c t) -> p c t", c=KC),
                                                xT[0][:, :, cols].bitcast(F32),
                                                ALU.subtract).then_inc(fill_free[bank], 1)
                    elif kind == "C":
                        dve.wait_ge(fill_full, fill_count(b, f))
                        nc.vector.tensor_scalar(neg_max[:], fill_bank[0:GH * QT, bank, 0:P], -1.0, None,
                                                ALU.mult).then_inc(fill_free[bank], 1)

                def work(b, items):
                    transposed_in = {}
                    waiting = []
                    for item in items:
                        kind, g, i, f, high, bnn = item
                        if waiting and (kind in F_KINDS or kind in ("sc", "av", "norm")):
                            low_part(b, waiting.pop())
                        if kind == "LS":
                            wait_token_tile(dve, b, i)
                            if i >= 2:
                                dve.wait_ge(ln_stat_done, next_batch_tiles(b, i) - 1)
                            nc.vector.bn_stats(bn[:, i % 2], token_tile(b, i)).then_inc(bn_done, 1)
                            dve.wait_ge(bn_done, bn_count(b, bnn))
                            dve.sem_inc(dve_passed, 1)
                            nc.vector.bn_aggr(ln_stat[:, i], bn[:, i % 2]).then_inc(ln_stat_done, 1)
                        elif kind == "LA":
                            if i == 0:
                                dve.wait_ge(rstd_done, 1 if b is None else b + 2)
                            if i >= 2:
                                dve.wait_ge(fill_full, fill_count(b, transposed_in[i - 2]))
                            wait_token_tile(dve, b, QT + i)
                            nc.vector.tensor_scalar(x_norm[:, i % 2], token_tile(b, i), ln_stat[:, i, 0:1],
                                                    rstd[:, i:i + 1], ALU.subtract,
                                                    ALU.mult).then_inc(x_norm_done, 1)
                        elif kind == "LB":
                            transposed_in[i] = f
                            waiting.append(item)
                        elif kind == "P" and is_last_piece(kind, i) and i[0] < 4:
                            waiting.append(item)
                        elif kind == "M":
                            bn_, gn = after(b, g)
                            h, qt, kc, n, _ = MAX_UNITS[i]
                            col = h * QT + qt
                            dve.wait_ge(max_full, per_group(bn_, gn, NM, i + 1))
                            nc.vector.tensor_reduce(maxima[:, kc, col:col + 1], max_bank[:, i % 2, 0:n],
                                                    AX.X, ALU.max).then_inc(max_free, 1)
                        elif kind == "C":
                            dve.wait_ge(max_free, per_group(*after(b, g), NM, NM + 2))
                            nc.vector.tensor_reduce(row_max[:], maxima[:].rearrange("p a n -> p n a"), AX.X,
                                                    ALU.max).then_inc(row_ready, 1)
                            waiting.append(item)
                        elif kind == "norm":
                            half, quarter = divmod(i, QUARTERS)
                            if quarter == 0:
                                dve.wait_ge(den_out, per_group(b, g, 2, half + 2))
                            part = den[:, half, quarter * P:(quarter + 1) * P]
                            nc.vector.reciprocal(part, part).then_inc(rec_done, 1)
                        elif kind == "O":
                            bank, before = fill_no(b, f)
                            x2 = x_res[:, i % 4]
                            if i == 0:
                                dve.wait_ge(stats_saved, b + 1)
                            if i >= 2:
                                dve.wait_ge(x2_stat_done, b * QT + (i - 1))
                            dve.wait_ge(x_res_full[i % 4], b * 32 + 16 * (i // 4 + 1))
                            dve.wait_ge(fill_full, fill_count(b, f))
                            nc.vector.tensor_tensor(x2, fill_bank[:, bank], x2, ALU.add).then_inc(x2_done, 1)
                            dve.wait_ge(x2_done, b * QT + (i + 1))
                            dve.sem_inc(fill_free[bank], 1)
                            nc.vector.bn_stats(bn[:, i % 2], x2).then_inc(bn_done, 1)
                            nc.vector.tensor_reduce(x2_stat[:, i, 2:3], x2, AX.X, ALU.max)
                            nc.vector.tensor_reduce(x2_stat[:, i, 3:4], x2, AX.X, ALU.min)
                            dve.wait_ge(bn_done, bn_count(b, bnn))
                            dve.sem_inc(dve_passed, 1)
                            nc.vector.bn_aggr(x2_stat[:, i, 0:2], bn[:, i % 2]).then_inc(x2_stat_done, 1)
                        elif kind == "stats":
                            dve.wait_ge(x2_stat_done, b * QT + QT)
                            nc.vector.tensor_copy(stats_all[:, bass.ds(b * QT, QT), :],
                                                  x2_stat[:]).then_inc(stats_saved, 1)
                    if waiting:
                        low_part(b, waiting.pop())

                dve.sem_inc(den_done, 1)
                dve.sem_inc(av_done, NS)
                run(dve, work)

            @block.sync
            def _(sp):
                def load_x(b, i):
                    sp.sem_inc(sp_passed, 1)
                    sp.dma_start(x_in[:, i % 2], x_t[bass.ds(next_batch_tiles(b, i), 1)].rearrange(
                        "o p d -> p (o d)")).then_inc(x_in_full[i % 2], 16)

                for k in range(4):
                    sp.sem_inc(x2_stored[k], 1)

                def load_residual(b, i):
                    sp.sem_inc(sp_passed, 1)
                    sp.dma_start(x_res[:, i % 4], x_t[bass.ds(b * QT + i, 1)].rearrange(
                        "o p d -> p (o d)")).then_inc(x_res_full[i % 4], 16)

                def stack_unit(group, unit):
                    bn_, gn = group
                    w, half = PROJECTIONS[unit]
                    sp.wait_ge(parked[unit % 2], per_group(bn_, gn, 2 * 16, (unit // 2 + 1) * 16))
                    for n, part in enumerate(((0, 1, 0), (0, 0, 1))[w]):
                        sp.dma_start((Qs, Ks)[w][n * HD:(n + 1) * HD, gn % 2, :,
                                                 half * HALF:(half + 1) * HALF].bitcast(F32),
                                     qk_scratch[unit, part].rearrange("(h c) t -> c h t", h=GH)
                                     ).then_inc(stacked[unit % 2], 16)

                def work(b, items):
                    if b is None:
                        for half in range(2):
                            sp.dma_start(probs[:, half], x_t[half * GH:(half + 1) * GH].rearrange("t p d -> p t d")
                                         ).then_inc(x_first_in[half], 16)
                        sp.dma_start(w_group[:, 0:4].bitcast(F32), w_scratch[0, :, 0:4]).then_inc(w_qk_in, 16)
                        sp.dma_start(w_group[:, 4:6].bitcast(F32), w_scratch[0, :, 4:6]).then_inc(w_v_in, 16)
                    for kind, g, i, f, high, bnn in items:
                        if kind in F_KINDS:
                            bank, before = fill_no(b, f)
                        next_weights = items is not LAST_ITEMS or g < G - 2
                        if kind == "P" and is_last_piece(kind, i) and i[0] < 4:
                            unit, _, ahead = i
                            w = PROJECTIONS[unit][0]
                            bn_, gn = after(b, g, ahead)
                            if not (b is None and ahead == 1):
                                sp.wait_ge(stacked[unit % 2], per_group(bn_, gn, 2 * UNIT_DMAS,
                                                                        (unit // 2 - 1) * UNIT_DMAS))
                            if g >= 0 and w == 0:
                                taken = GH * (FIRST[1] + TPH) if ahead == 2 else 1
                                sp.wait_ge(scored, per_group(b, g, GH * NS, taken))
                            sp.wait_ge(fill_free[bank], before + 2)
                            sp.dma_start(qk_scratch[unit].rearrange("a p t -> p a t"),
                                         qk_part[:, unit % 2].bitcast(F32)).then_inc(parked[unit % 2], 16)
                            if w == 1:
                                stack_unit((bn_, gn), unit - 1)
                                stack_unit((bn_, gn), unit)
                            if unit == 3 and next_weights:
                                sp.dma_start(w_group[:, 0:4].bitcast(F32),
                                             w_scratch[(g + 2) % G, :, 0:4]).then_inc(w_qk_in, 16)
                        elif kind == "P" and i == (5, PIECES - 1, 1) and next_weights:
                            sp.wait_ge(fill_full, fill_count(b, f))
                            sp.dma_start(w_group[:, 4:6].bitcast(F32),
                                         w_scratch[(g + 2) % G, :, 4:6]).then_inc(w_v_in, 16)
                        elif kind == "C":
                            gn = after(b, g)[1]
                            sp.wait_ge(fill_free[bank], before + 2)
                            for h in range(GH):
                                sp.dma_start(
                                    Qs[KROWS:KROWS + 1, gn % 2, h, :].bitcast(F32).rearrange("p (t q) -> p t q", t=QT),
                                    neg_max[h * QT:(h + 1) * QT, :].bitcast(F32)).then_inc(rows_in, 16)
                        elif kind == "LS" and b is not None:
                            sp.wait_ge(bn_done, bn_count(b, bnn))
                            load_x(b, (i + 2) % QT)
                        elif kind == "LA" and b is not None and i + 2 < QT:
                            sp.wait_ge(x_norm_done, next_batch_tiles(b, i) + 1)
                            load_x(b, i + 2)
                        elif kind == "sc" and g == 0 and i == (0, 0) and items is ITEMS:
                            sp.wait_ge(x_norm_done, b * QT + QT)
                            load_x(b, 0)
                            load_x(b, 1)
                        elif kind == "sc" and g == G - 1 and i == (0, 0):
                            for k in range(4):
                                sp.wait_ge(x2_stored[k], b * 32 + 1)
                                sp.sem_inc(sp_passed, 1)
                            sp.wait_ge(stats_saved, b + 1)
                            for k in range(4):
                                load_residual(b, k)
                        elif kind == "O":
                            sp.wait_ge(x2_done, b * QT + (i + 1))
                            sp.sem_inc(sp_passed, 1)
                            sp.dma_start(x2_scratch[bass.ds(b * QT + i, 1)].rearrange("o p d -> p (o d)"),
                                         x_res[:, i % 4]).then_inc(x2_stored[i % 4], 16)
                            if 1 <= i <= 4:
                                sp.wait_ge(x2_stored[i - 1], b * 32 + 17)
                                sp.sem_inc(sp_passed, 1)
                                sp.wait_ge(x2_stat_done, b * QT + i)
                                load_residual(b, i + 3)
                run(sp, work)
                for k in range(4):
                    sp.wait_ge(x2_stored[k], 32 * B + 1)


def linear_block(nc, sb, pb, sem, x2_scratch, fw_scratch, fw_inverse, ffn_b, out_t, ident_bf, stats_all):
    UT = 2
    UNITS = TILES // UT
    SLOTS = 8
    COLUMNS_DONE = 9
    AHEAD = 5
    with ExitStack() as mem:
        w_T = sb(mem, "f_wT", [P, KC, D], BF16)
        bias = sb(mem, "f_bias", [P, D])
        dev = sb(mem, "f_dev", [P, 3, TILES])
        minus_half = sb(mem, "f_minus_half", [P, TILES])
        rstd = sb(mem, "f_rstd", [P, TILES])
        mul_col = sb(mem, "f_mul", [P, TILES])
        add_col = sb(mem, "f_add", [P, TILES])
        part_max = sb(mem, "f_part_max", [P, 1])
        amax = sb(mem, "f_amax", [P, 1])
        scale = sb(mem, "f_scale", [P, 1])
        inverse = sb(mem, "f_inverse", [P, 1])
        back = sb(mem, "f_back", [P, 1])
        x2 = sb(mem, "f_x2", [P, SLOTS, UT, D])
        z = sb(mem, "f_z", [P, 2, UT, D])
        power = sb(mem, "f_power", [P, 2, UT, D])
        zq = sb(mem, "f_zq", [P, 2, UT, D], BF16)
        zT = sb(mem, "f_zT", [P, UT, KC, P], BF16)
        y = sb(mem, "f_y", [P, 2, UT, D], BF16)
        t_bank = pb(mem, "f_t_bank", [P, UT, 2 * HALF], BF16)
        o_bank = pb(mem, "f_o_bank", [P, 2 * UT, D])

        w_in, b_in = sem("f_w_in"), sem("f_b_in")
        small = sem("f_small")
        const, eps_out, rstd_out, all_max = sem("f_const"), sem("f_eps"), sem("f_rstd"), sem("f_all_max")
        x2_in = [sem(f"f_x2_in{k}") for k in range(SLOTS)]
        z_done = sem("f_z_done")
        p_done = sem("f_p_done")
        r_done = sem("f_r_done")
        q_done = sem("f_q_done")
        t_full, t_out = sem("f_t_full"), sem("f_t_out")
        o_full, o_out = sem("f_o_full"), sem("f_o_out")
        y_done = sem("f_y_done")
        stored = [sem(f"f_stored{k}") for k in range(SLOTS)]
        sp_passed = sem("f_sp_passed")

        def run(eng, step, lag):
            for k in range(SLOTS):
                step(0, k)
            with eng.Fori(1, UNITS // SLOTS) as i:
                for k in range(SLOTS):
                    step(i, k)
            for k in range(lag):
                step(UNITS // SLOTS, k)

        def number(i, k):
            n = i * SLOTS + k
            return None if isinstance(n, int) and not 0 <= n < UNITS else n

        with nc.Block() as block:
            @block.sync
            def _(sp):
                sp.dma_start(w_T[:], fw_scratch[:]).then_inc(w_in, 16)
                sp.dma_start(bias[:], ffn_b.rearrange("(o n) -> o n", o=1).broadcast_to((P, D))).then_inc(b_in, 16)

                def load(i, k):
                    sp.sem_inc(sp_passed, 1)
                    sp.dma_start(x2[:, k % SLOTS],
                                 x2_scratch[bass.ds((i * SLOTS + k) * UT, UT)].rearrange("t p d -> p t d")
                                 ).then_inc(x2_in[k % SLOTS], 16)

                def step(i, k):
                    wraps = k >= SLOTS - AHEAD
                    if not (isinstance(i, int) and i == UNITS // SLOTS - 1 and wraps):
                        if not (isinstance(i, int) and i == 0 and not wraps):
                            sp.wait_ge(stored[(k + AHEAD) % SLOTS], i * 16 + 16 * wraps)
                        load(i, k + AHEAD)
                    sp.wait_ge(y_done, i * SLOTS + (k + 1))
                    sp.sem_inc(sp_passed, 1)
                    sp.dma_start(out_t[bass.ds((i * SLOTS + k) * UT, UT)].rearrange("t p d -> p t d"),
                                 x2[:, k]).then_inc(stored[k], 16)
                for k in range(AHEAD):
                    load(0, k)
                for k in range(SLOTS):
                    step(0, k)
                with sp.Fori(1, UNITS // SLOTS - 1) as i:
                    for k in range(SLOTS):
                        step(i, k)
                for k in range(SLOTS):
                    step(UNITS // SLOTS - 1, k)
                for k in range(SLOTS):
                    sp.wait_ge(stored[k], 16 * UNITS // SLOTS)

            @block.gpsimd
            def _(pool):
                nc.gpsimd.memset(minus_half[:], -0.5)
                nc.gpsimd.tensor_scalar(rstd[:], stats_all[:, :, 1], EPS, None, ALU.add).then_inc(eps_out, 1)
                pool.wait_ge(eps_out, 1)
                nc.gpsimd.tensor_tensor(rstd[:], rstd[:], minus_half[:], ALU.pow).then_inc(rstd_out, 1)
                pool.wait_ge(small, 4)
                nc.gpsimd.partition_all_reduce(amax[:], part_max[:], P, RMAX).then_inc(all_max, 1)

                def step(i, k):
                    u = number(i, k)
                    if u is not None:
                        pool.wait_ge(p_done, u * 3 + 3)
                        if not (isinstance(u, int) and u < 2):
                            pool.wait_ge(t_full, u * UT - UT)
                        nc.gpsimd.tensor_tensor(zq[:, k % 2], z[:, k % 2], power[:, k % 2],
                                                ALU.subtract).then_inc(r_done, 1)
                    u = number(i, k - 2)
                    if u is not None:
                        pool.wait_ge(o_out, u * UT + UT)
                        slot = x2[:, (k - 2) % SLOTS]
                        nc.gpsimd.tensor_tensor(slot, slot, y[:, k % 2], ALU.add).then_inc(y_done, 1)
                run(pool, step, 2)

            @block.vector
            def _(dve):
                done = [0]

                def chained(ins):
                    done[0] += 1
                    ins.then_inc(small, 1)
                    dve.wait_ge(small, done[0])

                mean, largest, least = stats_all[:, :, 0], stats_all[:, :, 2], stats_all[:, :, 3]
                nc.vector.tensor_tensor(dev[:, 0], largest, mean, ALU.subtract)
                chained(nc.vector.tensor_tensor(dev[:, 1], mean, least, ALU.subtract))
                chained(nc.vector.tensor_tensor(dev[:, 0], dev[:, 0], dev[:, 1], ALU.max))
                dve.wait_ge(rstd_out, 1)
                chained(nc.vector.tensor_tensor(dev[:, 0], dev[:, 0], rstd[:], ALU.mult))
                chained(nc.vector.tensor_reduce(part_max[:], dev[:, 0], AX.X, ALU.max))
                dve.wait_ge(all_max, 1)
                chained(nc.vector.tensor_scalar(amax[:], amax[:], 1e-12, None, ALU.max))
                chained(nc.vector.reciprocal(scale[:], amax[:]))
                chained(nc.vector.tensor_scalar(scale[:], scale[:], FP8_MAX, FP8_MAX, ALU.mult, ALU.min))
                chained(nc.vector.tensor_scalar(mul_col[:], rstd[:], scale[:], None, ALU.mult))
                chained(nc.vector.scalar_tensor_tensor(out=add_col[:], in0=mean, scalar=-1.0, in1=mul_col[:],
                                                       op0=ALU.mult, op1=ALU.mult))
                assert done[0] == COLUMNS_DONE
                chained(nc.vector.reciprocal(inverse[:], scale[:]))
                chained(nc.vector.tensor_tensor(back[:], inverse[:], fw_inverse[:], ALU.mult))
                dve.wait_ge(b_in, 16)

                def step(i, k):
                    u = number(i, k)
                    if u is not None:
                        zk = z[:, k % 2].rearrange("p t d -> p (t d)")
                        pk = power[:, k % 2].rearrange("p t d -> p (t d)")
                        dve.wait_ge(z_done, u + 1)
                        nc.vector.tensor_scalar(pk.bitcast(U32), zk.bitcast(U32), EXPONENT, None,
                                                ALU.bitwise_and).then_inc(p_done, 1)
                        dve.wait_ge(p_done, u * 3 + 1)
                        nc.vector.tensor_scalar(pk, pk, SMALLEST, MAGIC, ALU.max, ALU.mult).then_inc(p_done, 1)
                        dve.wait_ge(p_done, u * 3 + 2)
                        nc.vector.tensor_tensor(zk, zk, pk, ALU.add).then_inc(p_done, 1)
                    u = number(i, k - 1)
                    if u is not None:
                        dve.wait_ge(r_done, u + 1)
                        rounded = zq[:, (k - 1) % 2].rearrange("p t d -> p (t d)")
                        nc.vector.tensor_scalar(rounded, rounded, FP8_MAX, -FP8_MAX, ALU.min,
                                                ALU.max).then_inc(q_done, 1)
                    u = number(i, k - 2)
                    if u is not None:
                        if not (isinstance(u, int) and u < 2):
                            dve.wait_ge(y_done, u - 1)
                        for t in range(UT):
                            dve.wait_ge(o_full, u * UT + (t + 1))
                            nc.vector.scalar_tensor_tensor(out=y[:, k % 2, t], in0=o_bank[:, k % 2 * UT + t],
                                                           scalar=back[:], in1=bias[:], op0=ALU.mult,
                                                           op1=ALU.add).then_inc(o_out, 1)
                run(dve, step, 2)

            @block.tensor
            def _(pe):
                pe.wait_ge(w_in, 16)

                def step(i, k):
                    u = number(i, k - 1)
                    if u is None:
                        return
                    for t in range(UT):
                        if t == 0:
                            pe.wait_ge(q_done, u + 1)
                        if not (isinstance(u, int) and u < 1):
                            pe.wait_ge(t_out, u * UT + (t + 1 - UT))
                        for c in range(KC):
                            last = nc.tensor.transpose(t_bank[:, t, c * P:(c + 1) * P],
                                                       zq[:, (k - 1) % 2, t, c * P:(c + 1) * P], ident_bf[:])
                        last.then_inc(t_full, 1)
                    for t in range(UT):
                        pe.wait_ge(t_out, u * UT + (t + 1))
                        if not (isinstance(u, int) and u < 2):
                            pe.wait_ge(o_out, u * UT + (t + 1 - 2 * UT))
                        for c in range(KC):
                            last = nc.tensor.matmul(o_bank[:, (k - 1) % 2 * UT + t], zT[:, t, c], w_T[:, c],
                                                    start=c == 0, stop=c == KC - 1)
                        last.then_inc(o_full, 1)
                run(pe, step, 1)

            @block.scalar
            def _(act):
                def step(i, k):
                    u = number(i, k)
                    if u is not None:
                        act.wait_ge(x2_in[k], i * 16 + 16)
                        if not (isinstance(u, int) and u < 2):
                            act.wait_ge(r_done, u - 1)
                        for t in range(UT):
                            col = bass.ds(u * UT + t, 1)
                            last = nc.scalar.activation(z[:, k % 2, t], x2[:, k, t], ACT.Identity,
                                                        bias=add_col[:, col], scale=mul_col[:, col])
                        last.then_inc(z_done, 1)
                    u = number(i, k - 1)
                    if u is not None:
                        for t in range(UT):
                            act.wait_ge(t_full, u * UT + (t + 1))
                            if not (isinstance(u, int) and u < 1):
                                act.wait_ge(o_full, u * UT + (t + 1 - UT))
                            nc.scalar.activation(zT[:, t].rearrange("p c t -> p (c t)"), t_bank[:, t, 0:D],
                                                 ACT.Copy).then_inc(t_out, 1)
                act.wait_ge(small, COLUMNS_DONE)
                run(act, step, 1)


_INS = ["L0_attn_x", "L0_attn_q_proj_weight", "L0_attn_k_proj_weight", "L0_attn_v_proj_weight",
        "L0_attn_o_proj_weight", "L0_ffn_weight", "L0_ffn_bias"]


def kernel(**inputs):
    import numpy as _np
    import concourse.bacc as _bacc
    from concourse.bass_utils import run_bass_kernel_spmd as _run

    nc = _bacc.Bacc("TRN2", target_bir_lowering=False, num_devices=1)
    arrays, args = {}, []
    for name in _INS:
        a = _np.ascontiguousarray(inputs[name])
        arrays[f"in_{name}"] = a
        args.append(nc.dram_tensor(f"in_{name}", a.shape, mybir.dt.from_np(a.dtype), kind="ExternalInput").ap())
    out = nc.dram_tensor("out_x", (B, S, D), F32, kind="ExternalOutput").ap()
    nc.disable_value_cache = True
    build_kernel(nc, *args, out)
    r = _run(nc, [arrays], core_ids=[0])
    return r.results[0]["out_x"]
```

```python
from contextlib import ExitStack

import concourse.bass as bass
from concourse import mybir

F32 = mybir.dt.float32
F32R = mybir.dt.float32r
BF16 = mybir.dt.bfloat16
U32 = mybir.dt.uint32
ALU = mybir.AluOpType
ACT = mybir.ActivationFunctionType
AX = mybir.AxisListType

B, S, D = 8, 1024, 512
HEADS = 16
HD = D // HEADS
P = 128
GH = P // HD
G = HEADS // GH
KC = D // P
QT = S // P
HALF = 512
TPH = HALF // P
TILES = B * QT
SCALE = HD ** -0.5
EPS = 1e-5
NEG = -3.0e38
MASKED = -1.0e30
KROWS = 3 * HD

FP8_MAX = 448.0
SMALLEST = 2.0 ** -6
MAGIC = 1.5 * 2.0 ** 20
EXPONENT = 0x7F800000
RMAX = bass.bass_isa.ReduceOp.max
FW_STEPS = 14

STEPS = [(0, kt) for kt in range(TPH)] + [(1, kt) for kt in range(QT)]
NS = len(STEPS)
FIRST = (0, TPH)
LAST = (TPH - 1, NS - 1)


def first_column(s):
    qc, kt = STEPS[s]
    return max(0, kt - TPH * qc) * P


def on_diagonal(s):
    qc, kt = STEPS[s]
    return kt >= TPH * qc


RINGED = [s for s in range(NS) if s not in FIRST]
DIRECT = [s for s in range(NS) if STEPS[s][0] == 1 and on_diagonal(s)]
ADDED = [s for s in RINGED if s not in DIRECT]

MAX_UNITS = []
for half_of_q in range(2):
    for h in range(GH):
        for qt in range(half_of_q * TPH, (half_of_q + 1) * TPH):
            for kc in range(half_of_q + 1):
                last = kc == qt // TPH
                MAX_UNITS.append((h, qt, kc, (qt - TPH * kc + 1) * P if last else HALF, last))
NM = len(MAX_UNITS)
HALF_UNITS = GH * TPH

PROJECTIONS = [(0, 0), (1, 0), (0, 1), (1, 1), (2, 0), (2, 1)]
RING = 4
QUARTERS = 4
PIECES = KC


def spread(items, start, end):
    return [(start + (end - start) * (n + 0.5) / len(items), item) for n, item in enumerate(items)]


def projection(u, ahead=1):
    return [("P", (u, piece, ahead)) for piece in range(PIECES)]


AT = {"heads": (0, 0.348, 0.55, 0.8), "av": 0.334, "av_step": 0.08, "wait": 0.012, "pull": 0, "step": 10,
      "row": 0, "qk1": 0.13, "v": (0.231, 0.368), "early": (0.678, 0.741),
      "max": ((0.003, 0.3), (0.34, 0.88)), "late_qk0": 0.11, "late_qk1": 0.247,
      "late_max": ((0.26, 0.42), (0.447, 0.9)), "late_v": (0.321, 0.46), "ln_v": (0.221, 0.337),
      "norm": (0.02, 0.5), "last_norm": (0.874, 0.999), "ln": 0.493, "ln_step": 0.056}


def products(g, s):
    return [("head", g, (s, j)) for j in range(GH - 1)] + [("av", g, s)]


def engine_time(kind, i):
    if kind == "P":
        return 0.65, 0.6 if i[0] < 4 and is_last_piece(kind, i) else 0.0
    if kind == "sc":
        return (HALF - first_column(i[0])) / HALF * 0.213 + 0.06, 0.0
    if kind == "M":
        n = MAX_UNITS[i][3]
        return n / HALF * 0.213 + 0.06, n / HALF * 0.54 + 0.07
    if kind == "head":
        return (HALF - first_column(i[0])) / HALF * 0.233, 0.0
    if kind == "av":
        one = (HALF - first_column(i)) / HALF * 0.233
        return one * (1 + GH * (i in DIRECT)) + (0.93 if i == LAST[1] else 0.0), 0.0
    return {"den": (0.93, 0), "T": (0.43, 0), "LB": (0.43, 0.6), "LS": (0, 0.9),
            "norm": (0, 0.85), "C": (0.06, 0.3)}.get(kind, (0, 0))


def weave(others, maxima):
    order, read = [], []
    pe = act = dve = 0.0
    others, maxima = sorted(others, key=lambda x: x[0]), list(maxima)
    while others or maxima:
        take = bool(maxima) and not others
        if maxima and others:
            lead = others[0][0] - maxima[0][0]
            free = len(read) < RING or read[-RING] <= pe
            take = lead > AT["wait"] or (lead > -AT["pull"] and free)
        item = (maxima if take else others).pop(0)[1]
        on_pe, on_dve = engine_time(item[0], item[2])
        pe += on_pe
        if take or on_dve:
            dve = max(dve, pe) + on_dve
        if take:
            read.append(dve + 0.1)
        elif item[0] == "sc":
            act = max(act, pe) + 2 * on_pe
            read.append(act + 0.1)
        order.append(item)
    return order


def group_order(g, has_next):
    placed = []
    with_stats = has_next and g == G - 3
    with_ln = has_next and g == G - 2
    late_start = g == G - 1
    starts_after_next = g != G - 2
    length = [HALF + AT["step"] - first_column(s) for s in range(NS)]
    at = [sum(length[:s]) / sum(length) for s in range(NS + 1)]
    for s in range(NS):
        for j, share in enumerate(AT["heads"]):
            placed.append((at[s] + share * (at[s + 1] - at[s]), ("sc", g, (s, j))))
        late = [at[s] + (AT["av"] + AT["av_step"] * j) * (at[s + 1] - at[s]) for j in range(GH)]
        if s > 0:
            placed += zip(late, products(g, s - 1))
        elif g > 0:
            placed += zip(late, products(g - 1, NS - 1))
            placed += [(late[-1] + 1e-4, ("out", g - 1, 1)), (late[-1] + 2e-4, ("dout", g - 1, 1))]
        if s - 1 == LAST[0]:
            placed.append((late[-1] + 1e-4, ("out", g, 0)))
    placed += [(at[6] + 1e-3, ("den", g, 0)), (at[6] + 1.1e-3, ("dout", g, 0))]
    if g > 0:
        placed += spread([("norm", g - 1, i) for i in range(2 * QUARTERS)], *AT["norm"])
    if g == G - 1:
        placed += spread([("norm", g, i) for i in range(QUARTERS)], *AT["last_norm"])
    more = []
    if with_stats:
        more += spread([("LS", i) for i in range(QT)], 0.05, 0.90)
    if has_next or g < G - 1:
        if late_start:
            more += spread(projection(0) + projection(1), 0.0, AT["late_qk0"])
            more += spread(projection(2) + projection(3), AT["late_qk0"], AT["late_qk1"])
        else:
            more += spread(projection(2) + projection(3), 0.0, AT["qk1"])
        v0, v1 = AT["ln_v" if with_ln else "late_v" if late_start else "v"]
        more += spread(projection(4), v0, v0 + 0.08) + [(v0 + 0.12, ("T", 0))]
        more += spread(projection(5), v1, v1 + 0.08) + [(v1 + 0.12, ("T", 1))]
        if with_ln:
            more.append((0.1, ("LR", 0)))
            for i in range(QT):
                place = AT["ln"] + AT["ln_step"] * i
                more += [(place, ("LA", i)), (place + 0.75 * AT["ln_step"], ("LB", i))]
        elif starts_after_next:
            more += spread(projection(0, 2) + projection(1, 2), *AT["early"])
        for units, (start, end) in zip((range(HALF_UNITS), range(HALF_UNITS, NM)),
                                       AT["late_max" if late_start else "max"]):
            cost = [MAX_UNITS[i][3] + 70 for i in units]
            for n, i in enumerate(units):
                more.append((start + (end - start) * sum(cost[:n]) / sum(cost), ("M", i)))
        more.append((end + AT["row"], ("C", 0)))
    placed += [(place, (kind, g, i)) for place, (kind, i) in more if kind != "M"]
    return weave(placed, [(place, (kind, g, i)) for place, (kind, i) in more if kind == "M"])


def batch_order(has_next):
    order = []
    for g in range(G):
        order += group_order(g, has_next)
    order += products(G - 1, NS - 1) + [("out", G - 1, 1), ("dout", G - 1, 1)]
    order += [("O", G - 1, 0)] + [("norm", G - 1, i) for i in range(QUARTERS, 2 * QUARTERS)]
    order += [("O", G - 1, tt) for tt in range(1, QT)] + [("stats", G - 1, 0)]
    return order


def first_order():
    order = [("LS", -1, i) for i in range(QT)] + [("LR", -1, 0), ("LA", -1, 0)]
    for i in range(QT):
        order += ([("LA", -1, i + 1)] if i + 1 < QT else []) + [("LB", -1, i)]
        if i >= TPH - 1 and i < TPH + 1:
            order += [("P", -1, x) for _, x in projection(i - TPH + 1)]
    for u in (2, 3):
        order += [("P", -1, i) for _, i in projection(u)]
    more = [("M", i) for i in range(NM)]
    others = projection(4) + [("T", 0)] + projection(5) + [("T", 1)] + projection(0, 2) + projection(1, 2)
    merged = sorted(spread(more, 0, 1) + spread(others, 0, 0.8), key=lambda x: x[0])
    return order + [(kind, -1, i) for _, (kind, i) in merged] + [("C", -1, 0)]


F_KINDS = ("P", "T", "C", "LB", "O")


def is_last_piece(kind, i):
    return kind != "P" or i[1] == PIECES - 1


def counted(order):
    f = high = bn = 0
    out = []
    ringed = []
    open_unit = False
    for kind, g, i in order:
        assert not (open_unit and kind in F_KINDS and kind != "P")
        ring = None
        if kind in ("sc", "M"):
            ring = (len(ringed) % RING, ringed[-RING] if len(ringed) >= RING else None)
            ringed.append((kind, g, i))
        out.append((kind, g, i, f, high, bn, ring))
        if kind == "P":
            open_unit = not is_last_piece(kind, i)
        if is_last_piece(kind, i):
            f += kind in F_KINDS
            high += kind == "LB" or (kind == "P" and i[0] < 4)
            bn += kind in ("LS", "O")
    return out, (f, high, bn)


FIRST_ITEMS, BEFORE = counted(first_order())
ITEMS, PER_BATCH = counted(batch_order(True))
LAST_ITEMS, _ = counted(batch_order(False))
LAST_LN = {(place, half): next(f for kind, g, i, f, *_ in items if (kind, i) == ("LB", (half + 1) * TPH - 1))
           for place, items in ((-1, FIRST_ITEMS), (G - 1, ITEMS)) for half in range(2)}


def build_kernel(nc, x, wq, wk, wv, wo, ffn_w, ffn_b, out):
    x_t = x.rearrange("b (t p) d -> (b t) p d", p=P)
    out_t = out.rearrange("b (t p) d -> (b t) p d", p=P)
    w_scratch = nc.dram_tensor("w_scratch", (G, P, 6, KC, P), F32, kind="Internal").ap()
    x2_scratch = nc.dram_tensor("x2_scratch", (TILES, P, D), F32, kind="Internal").ap()
    fw_scratch = nc.dram_tensor("fw_scratch", (P, KC, D), BF16, kind="Internal").ap()
    qk_scratch = nc.dram_tensor("qk_scratch", (4, 2, P, HALF), F32, kind="Internal").ap()

    ctx = ExitStack()
    with ctx:
        def sb(where, name, shape, dt=F32):
            return where.enter_context(nc.sbuf_tensor(name, shape, dt))

        def pb(where, name, shape, dt=F32):
            return where.enter_context(nc.psum_tensor(name, shape, dt))

        def sem(name):
            return ctx.enter_context(nc.semaphore(name))

        ident = sb(ctx, "ident", [P, P])
        ident_bf = sb(ctx, "ident_bf", [P, P], BF16)
        wo_T = sb(ctx, "wo_T", [P, KC, D])
        stats_all = sb(ctx, "stats_all", [P, TILES, 4])
        probs = sb(ctx, "probs", [P, 2, GH, HALF])
        x_first_in = [sem(f"x_first_in{i}") for i in range(2)]
        rstd_all = sb(ctx, "rstd_all", [P, TILES])
        fw_inverse = sb(ctx, "fw_inverse", [P, 1])
        weights_block(nc, sb, pb, sem, (wq, wk, wv, wo), ffn_w, ident, ident_bf, wo_T, w_scratch, fw_scratch,
                      fw_inverse, x_t, probs, x_first_in)
        attention_block(nc, sb, pb, sem, x_t, x2_scratch, w_scratch, qk_scratch, ident, ident_bf, wo_T, stats_all,
                        rstd_all, probs, x_first_in)
        linear_block(nc, sb, pb, sem, x2_scratch, fw_scratch, fw_inverse, ffn_b, out_t, ident_bf, stats_all,
                     rstd_all)


def weights_block(nc, sb, pb, sem, weights, ffn_w, ident, ident_bf, wo_T, w_scratch, fw_scratch, fw_inverse,
                  x_t, probs, x_first_in):
    with ExitStack() as mem:
        fw = sb(mem, "fw", [P, KC, D])
        fw_power = sb(mem, "fw_power", [P, KC, D])
        fw_q = sb(mem, "fw_q", [P, KC, D], BF16)
        fw_T = sb(mem, "fw_T", [P, KC, D], BF16)
        fw_max = sb(mem, "fw_max", [P, 4])
        fw_scale = sb(mem, "fw_scale", [P, 1])
        fw_bank = pb(mem, "fw_bank", [P, 2, 2 * D], BF16)
        fw_in, fw_step, fw_all_max = sem("fw_in"), sem("fw_step"), sem("fw_all_max")
        fw_turned, fw_out, fw_stored = sem("fw_turned"), sem("fw_out"), sem("fw_stored")
        w_rows = sb(mem, "w_rows", [P, 4, KC, D])
        w_high = sb(mem, "w_high", [P, 3, KC, D], F32R)
        w_low = sb(mem, "w_low", [P, 3, KC, D], F32R)
        bank = pb(mem, "w_bank", [P, 2, D])
        rows_in = [sem(f"w_rows_in{w}") for w in range(4)]
        zeroed, made = sem("w_zeroed"), sem("w_ident_made")
        turned, high_out, low_out = sem("w_turned"), sem("w_high_out"), sem("w_low_out")
        stored = sem("w_stored")
        units = [(w, c) for w in range(4) for c in range(KC)]

        with nc.Block() as block:
            @block.sync
            def _(sp):
                for w in range(4):
                    sp.dma_start(w_rows[:, w], weights[w].rearrange("(t p) d -> p t d", p=P)).then_inc(rows_in[w], 16)
                    if w == 1:
                        sp.dma_start(fw[:], ffn_w.rearrange("(t p) d -> p t d", p=P)).then_inc(fw_in, 16)
                for half in range(2):
                    sp.dma_start(probs[:, half], x_t[half * GH:(half + 1) * GH].rearrange("t p d -> p t d")
                                 ).then_inc(x_first_in[half], 16)
                for w in range(3):
                    sp.wait_ge(low_out, KC * (w + 1))
                    for g in range(G):
                        for part, half in enumerate((w_high, w_low)):
                            sp.dma_start(w_scratch[g, :, 2 * w + part, :, :],
                                         half[:, w, :, g * P:(g + 1) * P].bitcast(F32)).then_inc(stored, 16)
                sp.wait_ge(fw_out, KC)
                sp.dma_start(fw_scratch[:], fw_T[:]).then_inc(fw_stored, 16)
                sp.wait_ge(stored, 16 * 3 * G * 2)
                sp.wait_ge(fw_stored, 16)

            @block.gpsimd
            def _(pool):
                nc.gpsimd.memset(ident[:], 0.0).then_inc(zeroed, 1)
                nc.gpsimd.memset(ident_bf[:], 0.0).then_inc(zeroed, 1)
                pool.wait_ge(zeroed, 2)
                for one in (ident, ident_bf):
                    nc.gpsimd.affine_select(out=one[:], in_=one[:], compare_op=ALU.not_equal, fill=1.0, base=0,
                                            pattern=[[-1, P]], channel_multiplier=1).then_inc(made, 1)
                pool.wait_ge(fw_step, 4)
                nc.gpsimd.partition_all_reduce(fw_max[:, 3:4], fw_max[:, 2:3], P, RMAX).then_inc(fw_all_max, 1)

            @block.tensor
            def _(pe):
                pe.wait_ge(made, 2)
                for n, (w, c) in enumerate(units):
                    pe.wait_ge(rows_in[w], 16)
                    if n >= 2:
                        if n - 2 < 3 * KC:
                            pe.wait_ge(low_out, n - 1)
                        else:
                            pe.wait_ge(high_out, n - 1)
                    for t in range(KC):
                        last = nc.tensor.transpose(bank[:, n % 2, t * P:(t + 1) * P],
                                                   w_rows[:, w, t, c * P:(c + 1) * P], ident[:])
                    last.then_inc(turned, 1)
                pe.wait_ge(fw_step, FW_STEPS)
                for c in range(KC):
                    if c >= 2:
                        pe.wait_ge(fw_out, c - 1)
                    for t in range(KC):
                        last = nc.tensor.transpose(fw_bank[:, c % 2, t * P:(t + 1) * P],
                                                   fw_q[:, t, c * P:(c + 1) * P], ident_bf[:])
                    last.then_inc(fw_turned, 1)

            @block.scalar
            def _(act):
                for n, (w, c) in enumerate(units):
                    act.wait_ge(turned, n + 1)
                    to = w_high[:, w, c] if w < 3 else wo_T[:, c]
                    nc.scalar.activation(to, bank[:, n % 2], ACT.Copy).then_inc(high_out, 1)
                for c in range(KC):
                    act.wait_ge(fw_turned, c + 1)
                    nc.scalar.activation(fw_T[:, c], fw_bank[:, c % 2, 0:D], ACT.Copy).then_inc(fw_out, 1)

            @block.vector
            def _(dve):
                done = [0]

                def chained(ins):
                    done[0] += 1
                    ins.then_inc(fw_step, 1)
                    dve.wait_ge(fw_step, done[0])

                all_w = fw[:].rearrange("p t d -> p (t d)")
                all_p = fw_power[:].rearrange("p t d -> p (t d)")
                for n, (w, c) in enumerate(units[:3 * KC]):
                    dve.wait_ge(high_out, n + 1)
                    nc.vector.tensor_tensor(w_low[:, w, c], bank[:, n % 2], w_high[:, w, c].bitcast(F32),
                                            ALU.subtract).then_inc(low_out, 1)
                    if n == 4:
                        dve.wait_ge(fw_in, 16)
                        chained(nc.vector.tensor_reduce(fw_max[:, 0:1], all_w, AX.X, ALU.max))
                    elif n == 5:
                        chained(nc.vector.tensor_reduce(fw_max[:, 1:2], all_w, AX.X, ALU.min))
                        chained(nc.vector.tensor_scalar(fw_max[:, 1:2], fw_max[:, 1:2], -1.0, None, ALU.mult))
                        chained(nc.vector.tensor_tensor(fw_max[:, 2:3], fw_max[:, 0:1], fw_max[:, 1:2], ALU.max))
                    elif n == 6:
                        dve.wait_ge(fw_all_max, 1)
                        chained(nc.vector.tensor_scalar(fw_max[:, 3:4], fw_max[:, 3:4], 1e-12, None, ALU.max))
                        chained(nc.vector.reciprocal(fw_scale[:], fw_max[:, 3:4]))
                        chained(nc.vector.tensor_scalar(fw_scale[:], fw_scale[:], FP8_MAX, FP8_MAX, ALU.mult,
                                                        ALU.min))
                        chained(nc.vector.reciprocal(fw_inverse[:], fw_scale[:]))
                        chained(nc.vector.tensor_scalar(all_w, all_w, fw_scale[:], None, ALU.mult))
                    elif n == 7:
                        chained(nc.vector.tensor_scalar(all_p.bitcast(U32), all_w.bitcast(U32), EXPONENT, None,
                                                        ALU.bitwise_and))
                    elif n == 8:
                        chained(nc.vector.tensor_scalar(all_p, all_p, SMALLEST, MAGIC, ALU.max, ALU.mult))
                    elif n == 9:
                        chained(nc.vector.tensor_tensor(all_w, all_w, all_p, ALU.add))
                    elif n == 10:
                        chained(nc.vector.tensor_tensor(all_w, all_w, all_p, ALU.subtract))
                    elif n == 11:
                        chained(nc.vector.tensor_scalar(fw_q[:].rearrange("p t d -> p (t d)"), all_w, FP8_MAX,
                                                        -FP8_MAX, ALU.min, ALU.max))
                assert done[0] == FW_STEPS


def attention_block(nc, sb, pb, sem, x_t, x2_scratch, w_scratch, qk_scratch, ident, ident_bf, wo_T, stats_all,
                    rstd_all, probs, x_first_in):
    with ExitStack() as mem:
        xT = [sb(mem, f"xT_{part}", [P, KC, S], F32R) for part in ("high", "low")]
        w_group = sb(mem, "w_group", [P, 6, KC, P], F32R)
        qk_part = sb(mem, "qk_part", [P, 2, 2, HALF], F32R)
        vT = sb(mem, "vT", [P, HALF])
        v_group = sb(mem, "v_group", [P, 2, QT, P])
        Qs = sb(mem, "Qs", [KROWS + 1, 2, GH, S], F32R)
        Ks = sb(mem, "Ks", [KROWS + 1, 2, GH, S], F32R)
        acc = sb(mem, "acc", [P, 2, GH, HALF])
        attn_T = sb(mem, "attn_T", [P, G, S])
        den = sb(mem, "den", [P, 2, HALF])
        x_in = sb(mem, "x_in", [P, 2, D])
        x_norm = sb(mem, "x_norm", [P, 2, D])
        x_res = sb(mem, "x_res", [P, 4, D])
        ones = sb(mem, "ones", [P, HD])
        mask = sb(mem, "mask", [P, P], BF16)
        mask_T = sb(mem, "mask_T", [P, P], BF16)
        maxima = sb(mem, "maxima", [P, 2, GH * QT])
        row_max = sb(mem, "row_max", [P, GH * QT])
        neg_max = sb(mem, "neg_max", [GH * QT, P], F32R)
        bn = sb(mem, "bn", [P, 2, 6])
        ln_stat = sb(mem, "ln_stat", [P, QT, 2])
        var_eps = sb(mem, "var_eps", [P, QT])
        rstd = sb(mem, "rstd", [P, QT])
        shift = sb(mem, "shift", [P, QT])
        minus_half = sb(mem, "minus_half", [P, QT])
        x2_stat = sb(mem, "x2_stat", [P, QT, 4])
        x2_var = sb(mem, "x2_var", [P, QT])

        ring_bank = pb(mem, "ring_bank", [P, RING, HALF])
        fill_bank = pb(mem, "fill_bank", [P, 2, HALF])
        av_bank = pb(mem, "av_bank", [P, HALF])
        den_bank = pb(mem, "den_bank", [P, HALF])

        consts = sem("consts")
        ones_row = sem("ones_row")
        pool_passed, dve_passed, sp_passed = sem("pool_passed"), sem("dve_passed"), sem("sp_passed")
        scored = sem("scored")
        exp_done = sem("exp_done")
        added = sem("added")
        av_done = sem("av_done")
        den_done = sem("den_done")
        den_out = sem("den_out")
        rec_done = sem("rec_done")
        av_out = sem("av_out")
        normed = sem("normed")
        max_full = sem("max_full")
        max_free = sem("max_free")
        row_ready = sem("row_ready")
        fill_full = sem("fill_full")
        fill_free = [sem(f"fill_free{i}") for i in range(2)]
        high_done = sem("high_done")
        vT_done = sem("vT_done")
        v_done = sem("v_done")
        parked = [sem(f"parked{i}") for i in range(2)]
        stacked = [sem(f"stacked{i}") for i in range(2)]
        rows_in = sem("rows_in")
        w_qk_in, w_v_in = sem("w_qk_in"), sem("w_v_in")
        x_in_full = [sem(f"x_in_full{i}") for i in range(2)]
        bn_done = sem("bn_done")
        ln_stat_done = sem("ln_stat_done")
        eps_done = sem("eps_done")
        rstd_done = sem("rstd_done")
        x_norm_done = sem("x_norm_done")
        x_res_full = [sem(f"x_res_full{i}") for i in range(4)]
        x2_done = sem("x2_done")
        x2_stat_done = sem("x2_stat_done")
        x2_eps_done = sem("x2_eps_done")
        x2_rstd_done = sem("x2_rstd_done")
        stats_saved = sem("stats_saved")
        x2_stored = [sem(f"x2_stored{i}") for i in range(4)]

        UNIT_DMAS = 16 * 3

        def fill_no(b, f):
            if b is None:
                return f % 2, f // 2
            return (BEFORE[0] + f) % 2, b * (PER_BATCH[0] // 2) + (BEFORE[0] + f) // 2

        def fill_count(b, f):
            return f + 1 if b is None else b * PER_BATCH[0] + (BEFORE[0] + f + 1)

        def high_count(b, h):
            return h + 1 if b is None else b * PER_BATCH[1] + (BEFORE[1] + h + 1)

        def bn_count(b, n):
            return n + 1 if b is None else b * PER_BATCH[2] + (BEFORE[2] + n + 1)

        def per_group(b, g, each, more):
            return (0 if b is None else b * (each * G)) + (each * g + more)

        def after(b, g, ahead=1):
            return (0, ahead - 1) if b is None else (b, g + ahead)

        def next_batch_tiles(b, i):
            return i if b is None else b * QT + (QT + i)

        def token_tile(b, i):
            return probs[:, i // GH, i % GH] if b is None else x_in[:, i % 2]

        def wait_token_tile(eng, b, n):
            if b is None:
                eng.wait_ge(x_first_in[n % QT // GH], 16)
            else:
                eng.wait_ge(x_in_full[n % 2], b * (16 * QT) + 16 * (n // 2 + 1))

        def run(eng, body):
            body(None, FIRST_ITEMS)
            with eng.Fori(0, B - 1) as b:
                body(b, ITEMS)
            body(B - 1, LAST_ITEMS)

        with nc.Block() as block:
            @block.gpsimd
            def _(pool):
                nc.gpsimd.memset(ones[:], 1.0)
                nc.gpsimd.memset(minus_half[:], -0.5)
                nc.gpsimd.memset(maxima[:], NEG)
                nc.gpsimd.memset(mask_T[:], 0.0)
                nc.gpsimd.memset(mask[:], 0.0).then_inc(consts, 1)
                pool.wait_ge(consts, 1)
                nc.gpsimd.affine_select(out=mask[:], in_=mask[:], compare_op=ALU.is_ge, fill=MASKED, base=0,
                                        pattern=[[-1, P]], channel_multiplier=1).then_inc(consts, 1)
                nc.gpsimd.affine_select(out=mask_T[:], in_=mask_T[:], compare_op=ALU.is_ge, fill=MASKED, base=0,
                                        pattern=[[1, P]], channel_multiplier=-1).then_inc(consts, 1)
                pool.wait_ge(consts, 3)
                nc.gpsimd.memset(Ks[KROWS:KROWS + 1].bitcast(F32), 1.0).then_inc(ones_row, 1)
                pool.wait_ge(ones_row, 1)

                def work(b, items):
                    for kind, g, i, f, high, bnn, ring in items:
                        if kind == "LR":
                            n = next_batch_tiles(b, 0)
                            if b is not None:
                                pool.wait_ge(rstd_done, b + 1)
                                pool.wait_ge(x_norm_done, n)
                            pool.wait_ge(ln_stat_done, n + QT)
                            pool.sem_inc(pool_passed, 1)
                            nc.gpsimd.tensor_scalar(var_eps[:], ln_stat[:, :, 1], EPS, None,
                                                    ALU.add).then_inc(eps_done, 1)
                            pool.wait_ge(eps_done, 1 if b is None else 3 * b + 4)
                            pool.sem_inc(pool_passed, 1)
                            nc.gpsimd.tensor_tensor(rstd[:], var_eps[:], minus_half[:],
                                                    ALU.pow).then_inc(eps_done, 1)
                            pool.wait_ge(eps_done, 2 if b is None else 3 * b + 5)
                            pool.sem_inc(pool_passed, 1)
                            nc.gpsimd.tensor_scalar(var_eps[:], rstd[:], -1.0, None, ALU.mult).then_inc(eps_done, 1)
                            pool.wait_ge(eps_done, 3 if b is None else 3 * b + 6)
                            pool.sem_inc(pool_passed, 1)
                            nc.gpsimd.tensor_tensor(shift[:], ln_stat[:, :, 0], var_eps[:],
                                                    ALU.mult).then_inc(rstd_done, 1)
                        elif kind == "stats":
                            pool.wait_ge(x2_rstd_done, b + 1)
                            pool.wait_ge(x2_stat_done, b * QT + QT)
                            pool.sem_inc(pool_passed, 1)
                            nc.gpsimd.tensor_scalar(x2_var[:], x2_stat[:, :, 1], EPS, None,
                                                    ALU.add).then_inc(x2_eps_done, 1)
                            pool.wait_ge(x2_eps_done, b + 1)
                            pool.sem_inc(pool_passed, 1)
                            nc.gpsimd.tensor_tensor(rstd_all[:, bass.ds(b * QT, QT)], x2_var[:], minus_half[:],
                                                    ALU.pow).then_inc(x2_rstd_done, 1)
                        elif kind == "av" and i in ADDED:
                            qc = STEPS[i][0]
                            off = first_column(i)
                            pool.wait_ge(exp_done, per_group(b, g, GH * NS, GH * (i + 1) + 2))
                            pool.wait_ge(av_done, per_group(b, g, NS, FIRST[qc] + 1 + NS))
                            if ADDED.index(i) % (len(ADDED) // 2):
                                pool.wait_ge(added, per_group(b, g, len(ADDED), ADDED.index(i)))
                            for j in range(GH):
                                last = nc.gpsimd.tensor_tensor(acc[:, qc, j, off:], acc[:, qc, j, off:],
                                                               probs[:, RINGED.index(i) % 2, j, off:], ALU.add)
                            last.then_inc(added, 1)
                        elif kind == "norm" and i % QUARTERS == QUARTERS - 1:
                            half = i // QUARTERS
                            pool.wait_ge(rec_done, per_group(b, g, 2 * QUARTERS, i + 1))
                            pool.wait_ge(av_out, per_group(b, g, 2, half + 2))
                            part = attn_T[:, g, half * HALF:(half + 1) * HALF]
                            nc.gpsimd.tensor_tensor(part, part, den[:, half], ALU.mult).then_inc(normed, 1)
                pool.sem_inc(x2_rstd_done, 1)
                run(pool, work)

            @block.tensor
            def _(pe):
                pe.wait_ge(consts, 3)

                def fill_target(b, f):
                    bank, before = fill_no(b, f)
                    pe.wait_ge(fill_free[bank], before + 1)
                    return bank

                def ring_target(b, ring):
                    bank, before = ring
                    if before is None:
                        if b is not None:
                            pe.wait_ge(exp_done, per_group(b, 0, GH * NS, 2))
                            pe.wait_ge(max_free, per_group(b, 0, NM, NM))
                    elif before[0] == "sc":
                        _, g, (s, j) = before
                        pe.wait_ge(exp_done, per_group(b, g, GH * NS, GH * s + j + 1 + 2))
                    else:
                        _, g, i = before
                        pe.wait_ge(max_free, per_group(*after(b, g), NM, i + 1))
                    return bank

                def work(b, items):
                    for kind, g, i, f, high, bnn, ring in items:
                        if kind == "P":
                            unit, c, ahead = i
                            w, half = PROJECTIONS[unit]
                            if unit == 0 and c == 0:
                                pe.wait_ge(w_qk_in, per_group(*after(b, g, ahead), 16, 16))
                            if unit == 4 and c == 0:
                                pe.wait_ge(w_v_in, per_group(*after(b, g, ahead), 16, 16))
                            if i in ((0, 0, 1), (2, 0, 1)) and g in (-1, G - 1):
                                ln_bank, before = fill_no(b, LAST_LN[g, half])
                                pe.wait_ge(fill_free[ln_bank], before + 2)
                            bank = fill_target(b, f) if c == 0 else fill_no(b, f)[0]
                            cols = slice(half * HALF, (half + 1) * HALF)
                            for wp, xp in ((0, 0), (1, 0), (0, 1)):
                                last = nc.tensor.matmul(fill_bank[:, bank], w_group[:, 2 * w + wp, c],
                                                        xT[xp][:, c, cols], start=(c == 0 and wp + xp == 0),
                                                        stop=(c == KC - 1 and xp == 1))
                            if is_last_piece(kind, i):
                                last.then_inc(fill_full, 1)
                        elif kind == "T":
                            bank = fill_target(b, f)
                            pe.wait_ge(vT_done, per_group(*after(b, g), 2, i + 1))
                            for t in range(TPH):
                                last = nc.tensor.transpose(fill_bank[:, bank, t * P:(t + 1) * P],
                                                           vT[:, t * P:(t + 1) * P], ident[:])
                            last.then_inc(fill_full, 1)
                        elif kind == "M":
                            bn_, gn = after(b, g)
                            h, qt, kc, n, diagonal = MAX_UNITS[i]
                            if i == 0:
                                for slot in range(2):
                                    pe.wait_ge(stacked[slot], per_group(bn_, gn, 2 * UNIT_DMAS, UNIT_DMAS))
                            if i == GH * TPH:
                                for slot in range(2):
                                    pe.wait_ge(stacked[slot], per_group(bn_, gn, 2 * UNIT_DMAS, 2 * UNIT_DMAS))
                            bank = ring_target(b, ring)
                            last = nc.tensor.matmul(ring_bank[:, bank, 0:n],
                                                    Qs[0:KROWS, gn % 2, h, qt * P:(qt + 1) * P],
                                                    Ks[0:KROWS, gn % 2, h, kc * HALF:kc * HALF + n],
                                                    start=True, stop=not diagonal)
                            if diagonal:
                                last = nc.tensor.matmul(ring_bank[:, bank, n - P:n], ident_bf[:], mask[:],
                                                        start=False, stop=True)
                            last.then_inc(max_full, 1)
                        elif kind == "C":
                            bank = fill_target(b, f)
                            pe.wait_ge(row_ready, per_group(*after(b, g), 1, 1))
                            nc.tensor.transpose(fill_bank[0:GH * QT, bank, 0:P], row_max[:],
                                                ident[:]).then_inc(fill_full, 1)
                        elif kind == "LB":
                            bank = fill_target(b, f)
                            pe.wait_ge(x_norm_done, next_batch_tiles(b, i) + 1)
                            for c in range(KC):
                                last = nc.tensor.transpose(fill_bank[:, bank, c * P:(c + 1) * P],
                                                           x_norm[:, i % 2, c * P:(c + 1) * P], ident[:])
                            last.then_inc(fill_full, 1)
                        elif kind == "O":
                            bank = fill_target(b, f)
                            pe.wait_ge(normed, b * (2 * G) + (2 * G + 1 + i // TPH))
                            for c in range(G):
                                last = nc.tensor.matmul(fill_bank[:, bank], attn_T[:, c, i * P:(i + 1) * P],
                                                        wo_T[:, c], start=(c == 0), stop=(c == G - 1))
                            last.then_inc(fill_full, 1)
                        elif kind == "sc":
                            s, j = i
                            qc, kt = STEPS[s]
                            off = first_column(s)
                            if b is not None and s == 0 and j == 0 and g == 0:
                                pe.wait_ge(ones_row, 1)
                            if s == 0 and j == 0:
                                pe.wait_ge(rows_in, per_group(b, g, 16 * GH, 16 * GH))
                                pe.wait_ge(v_done, per_group(b, g, 2, 2))
                            bank = ring_target(b, ring)
                            q0 = qc * HALF
                            last = nc.tensor.matmul(ring_bank[:, bank, off:], Ks[:, g % 2, j, kt * P:(kt + 1) * P],
                                                    Qs[:, g % 2, j, q0 + off:q0 + HALF],
                                                    start=True, stop=not on_diagonal(s))
                            if on_diagonal(s):
                                last = nc.tensor.matmul(ring_bank[:, bank, off:off + P], ident_bf[:], mask_T[:],
                                                        start=False, stop=True)
                            last.then_inc(scored, 1)
                        elif kind in ("head", "av"):
                            i, j = i if kind == "head" else (i, GH - 1)
                            qc, kt = STEPS[i]
                            off = first_column(i)
                            half_no = per_group(b, g, 2, qc)
                            if i in FIRST and j == 0:
                                pe.wait_ge(av_out, half_no + 1)
                            pe.wait_ge(exp_done, per_group(b, g, GH * NS, GH * i + j + 1 + 2))
                            tile = acc[:, qc, j] if i in FIRST else probs[:, RINGED.index(i) % 2, j]
                            rows = slice(j * HD, (j + 1) * HD)
                            last = nc.tensor.matmul(av_bank[rows, off:], v_group[:, g % 2, kt, rows],
                                                    tile[:, off:], start=i in FIRST, stop=i in LAST)
                            if kind == "head":
                                continue
                            if i == DIRECT[0]:
                                pe.wait_ge(den_out, half_no + 1)
                            if i in DIRECT:
                                if i == LAST[1]:
                                    pe.wait_ge(added, per_group(b, g, len(ADDED), len(ADDED)))
                                    for j in range(GH):
                                        nc.tensor.matmul(den_bank[j * HD:(j + 1) * HD, :], ones[:], acc[:, 1, j],
                                                         start=False, stop=False)
                                for j in range(GH):
                                    last = nc.tensor.matmul(den_bank[j * HD:(j + 1) * HD, off:], ones[:],
                                                            probs[:, RINGED.index(i) % 2, j, off:],
                                                            start=i == DIRECT[0], stop=i == LAST[1])
                            last.then_inc(av_done, 1)
                        elif kind == "den":
                            pe.wait_ge(den_out, per_group(b, g, 2, 1))
                            pe.wait_ge(added, per_group(b, g, len(ADDED), TPH - 1))
                            for j in range(GH):
                                last = nc.tensor.matmul(den_bank[j * HD:(j + 1) * HD, :], ones[:], acc[:, 0, j],
                                                        start=True, stop=True)
                            last.then_inc(den_done, 1)
                run(pe, work)

            @block.scalar
            def _(act):
                act.sem_inc(exp_done, 2)
                act.sem_inc(av_out, 1)
                act.sem_inc(den_out, 1)

                def work(b, items):
                    transposed_in = {}
                    for kind, g, i, f, high, bnn, ring in items:
                        if kind in F_KINDS:
                            bank, before = fill_no(b, f)
                        if kind == "P" and is_last_piece(kind, i):
                            act.wait_ge(fill_full, fill_count(b, f))
                            unit, _, ahead = i
                            bn_, gn = after(b, g, ahead)
                            if unit < 4:
                                if not (g < 0 and unit < 2 and ahead == 1):
                                    act.wait_ge(parked[unit % 2], per_group(bn_, gn, 2 * 16, unit // 2 * 16))
                                nc.scalar.activation(qk_part[:, unit % 2, 0], fill_bank[:, bank],
                                                     ACT.Copy).then_inc(high_done, 1)
                            else:
                                nc.scalar.activation(vT[:], fill_bank[:, bank], ACT.Copy).then_inc(vT_done, 1)
                                act.wait_ge(vT_done, per_group(bn_, gn, 2, unit - 4 + 1))
                                act.sem_inc(fill_free[bank], 1)
                        elif kind == "T":
                            act.wait_ge(fill_full, fill_count(b, f))
                            gn = after(b, g)[1]
                            nc.scalar.activation(v_group[:, gn % 2, i * TPH:(i + 1) * TPH],
                                                 fill_bank[:, bank].rearrange("p (t c) -> p t c", t=TPH),
                                                 ACT.Copy).then_inc(v_done, 1)
                            act.wait_ge(v_done, per_group(*after(b, g), 2, i + 1))
                            act.sem_inc(fill_free[bank], 1)
                        elif kind == "LA":
                            if i == 0:
                                act.wait_ge(rstd_done, 1 if b is None else b + 2)
                            if i >= 2:
                                act.wait_ge(fill_full, fill_count(b, transposed_in[i - 2]))
                            wait_token_tile(act, b, QT + i)
                            nc.scalar.activation(x_norm[:, i % 2], token_tile(b, i), ACT.Identity,
                                                 bias=shift[:, i:i + 1], scale=rstd[:, i:i + 1]
                                                 ).then_inc(x_norm_done, 1)
                        elif kind == "LB":
                            transposed_in[i] = f
                            act.wait_ge(fill_full, fill_count(b, f))
                            nc.scalar.activation(xT[0][:, :, i * P:(i + 1) * P],
                                                 fill_bank[:, bank].rearrange("p (c t) -> p c t", c=KC),
                                                 ACT.Copy).then_inc(high_done, 1)
                        elif kind == "sc":
                            s, j = i
                            qc, kt = STEPS[s]
                            off = first_column(s)
                            if j == 0:
                                if s in FIRST:
                                    if qc == 0:
                                        act.wait_ge(den_done, per_group(b, g, 1, 1))
                                    else:
                                        act.wait_ge(av_done, per_group(b, g, NS, NS))
                                    tile_of = acc[:, qc]
                                else:
                                    k = RINGED.index(s)
                                    used = RINGED[k - 2] if k >= 2 else RINGED[k - 2] - NS
                                    act.wait_ge(av_done, per_group(b, g, NS, used + 1 + NS))
                                    if k >= 2 and used in ADDED:
                                        act.wait_ge(added, per_group(b, g, len(ADDED), ADDED.index(used) + 1))
                                    tile_of = probs[:, k % 2]
                            act.wait_ge(scored, per_group(b, g, GH * NS, GH * s + j + 1))
                            nc.scalar.activation(tile_of[:, j, off:], ring_bank[:, ring[0], off:], ACT.Exp,
                                                 scale=SCALE).then_inc(exp_done, 1)
                        elif kind == "dout":
                            if i == 0:
                                act.wait_ge(den_done, per_group(b, g, 1, 2))
                            else:
                                act.wait_ge(av_done, per_group(b, g, NS, NS + NS))
                            act.wait_ge(normed, per_group(b, g, 2, i + 1))
                            nc.scalar.activation(den[:, i], den_bank[:], ACT.Copy).then_inc(den_out, 1)
                        elif kind == "out":
                            act.wait_ge(av_done, per_group(b, g, NS, LAST[i] + 1 + NS))
                            nc.scalar.activation(attn_T[:, g, i * HALF:(i + 1) * HALF], av_bank[:],
                                                 ACT.Copy).then_inc(av_out, 1)
                run(act, work)

            @block.vector
            def _(dve):
                dve.sem_inc(normed, 2)
                dve.sem_inc(stats_saved, 1)
                dve.sem_inc(fill_free[0], 1)
                dve.sem_inc(fill_free[1], 1)
                dve.wait_ge(consts, 2)

                def low_part(b, item):
                    kind, g, i, f, high, bnn, ring = item
                    bank, before = fill_no(b, f)
                    if kind == "P":
                        slot = i[0] % 2
                        dve.wait_ge(high_done, high_count(b, high))
                        nc.vector.tensor_tensor(qk_part[:, slot, 1], fill_bank[:, bank],
                                                qk_part[:, slot, 0].bitcast(F32),
                                                ALU.subtract).then_inc(fill_free[bank], 1)
                    elif kind == "LB":
                        dve.wait_ge(high_done, high_count(b, high))
                        cols = slice(i * P, (i + 1) * P)
                        nc.vector.tensor_tensor(xT[1][:, :, cols],
                                                fill_bank[:, bank].rearrange("p (c t) -> p c t", c=KC),
                                                xT[0][:, :, cols].bitcast(F32),
                                                ALU.subtract).then_inc(fill_free[bank], 1)
                    elif kind == "C":
                        dve.wait_ge(fill_full, fill_count(b, f))
                        nc.vector.tensor_scalar(neg_max[:], fill_bank[0:GH * QT, bank, 0:P], -1.0, None,
                                                ALU.mult).then_inc(fill_free[bank], 1)

                def work(b, items):
                    waiting = []
                    for item in items:
                        kind, g, i, f, high, bnn, ring = item
                        if waiting and (kind in F_KINDS or kind in ("sc", "av", "norm")
                                        or (b is None and kind == "M")):
                            low_part(b, waiting.pop())
                        if kind == "LS":
                            if i == 0 and b is not None:
                                dve.wait_ge(rstd_done, b + 1)
                            wait_token_tile(dve, b, i)
                            if i >= 2:
                                dve.wait_ge(ln_stat_done, next_batch_tiles(b, i) - 1)
                            nc.vector.bn_stats(bn[:, i % 2], token_tile(b, i)).then_inc(bn_done, 1)
                            dve.wait_ge(bn_done, bn_count(b, bnn))
                            dve.sem_inc(dve_passed, 1)
                            nc.vector.bn_aggr(ln_stat[:, i], bn[:, i % 2]).then_inc(ln_stat_done, 1)
                        elif kind == "LB":
                            waiting.append(item)
                        elif kind == "P" and is_last_piece(kind, i) and i[0] < 4:
                            waiting.append(item)
                        elif kind == "M":
                            bn_, gn = after(b, g)
                            h, qt, kc, n, _ = MAX_UNITS[i]
                            col = h * QT + qt
                            dve.wait_ge(max_full, per_group(bn_, gn, NM, i + 1))
                            nc.vector.tensor_reduce(maxima[:, kc, col:col + 1], ring_bank[:, ring[0], 0:n],
                                                    AX.X, ALU.max).then_inc(max_free, 1)
                        elif kind == "C":
                            dve.wait_ge(max_free, per_group(*after(b, g), NM, NM))
                            nc.vector.tensor_reduce(row_max[:], maxima[:].rearrange("p a n -> p n a"), AX.X,
                                                    ALU.max).then_inc(row_ready, 1)
                            waiting.append(item)
                        elif kind == "norm":
                            half, quarter = divmod(i, QUARTERS)
                            if quarter == 0:
                                dve.wait_ge(den_out, per_group(b, g, 2, half + 2))
                            part = den[:, half, quarter * P:(quarter + 1) * P]
                            nc.vector.reciprocal(part, part).then_inc(rec_done, 1)
                        elif kind == "O":
                            bank, before = fill_no(b, f)
                            x2 = x_res[:, i % 4]
                            if i == 0:
                                dve.wait_ge(stats_saved, b + 1)
                                dve.wait_ge(x2_rstd_done, b + 1)
                            if i >= 2:
                                dve.wait_ge(x2_stat_done, b * QT + (i - 1))
                            dve.wait_ge(x_res_full[i % 4], b * 32 + 16 * (i // 4 + 1))
                            dve.wait_ge(fill_full, fill_count(b, f))
                            nc.vector.tensor_tensor(x2, fill_bank[:, bank], x2, ALU.add).then_inc(x2_done, 1)
                            dve.wait_ge(x2_done, b * QT + (i + 1))
                            dve.sem_inc(fill_free[bank], 1)
                            nc.vector.bn_stats(bn[:, i % 2], x2).then_inc(bn_done, 1)
                            nc.vector.tensor_reduce(x2_stat[:, i, 2:3], x2, AX.X, ALU.max)
                            nc.vector.tensor_reduce(x2_stat[:, i, 3:4], x2, AX.X, ALU.min)
                            dve.wait_ge(bn_done, bn_count(b, bnn))
                            dve.sem_inc(dve_passed, 1)
                            nc.vector.bn_aggr(x2_stat[:, i, 0:2], bn[:, i % 2]).then_inc(x2_stat_done, 1)
                        elif kind == "stats":
                            dve.wait_ge(x2_stat_done, b * QT + QT)
                            nc.vector.tensor_copy(stats_all[:, bass.ds(b * QT, QT), :],
                                                  x2_stat[:]).then_inc(stats_saved, 1)
                    if waiting:
                        low_part(b, waiting.pop())

                dve.sem_inc(den_done, 1)
                dve.sem_inc(av_done, NS)
                run(dve, work)

            @block.sync
            def _(sp):
                def load_x(b, i):
                    sp.sem_inc(sp_passed, 1)
                    sp.dma_start(x_in[:, i % 2], x_t[bass.ds(next_batch_tiles(b, i), 1)].rearrange(
                        "o p d -> p (o d)")).then_inc(x_in_full[i % 2], 16)

                for k in range(4):
                    sp.sem_inc(x2_stored[k], 1)

                def load_residual(b, i):
                    sp.sem_inc(sp_passed, 1)
                    sp.dma_start(x_res[:, i % 4], x_t[bass.ds(b * QT + i, 1)].rearrange(
                        "o p d -> p (o d)")).then_inc(x_res_full[i % 4], 16)

                def stack_unit(group, unit):
                    bn_, gn = group
                    w, half = PROJECTIONS[unit]
                    sp.wait_ge(parked[unit % 2], per_group(bn_, gn, 2 * 16, (unit // 2 + 1) * 16))
                    for n, part in enumerate(((0, 1, 0), (0, 0, 1))[w]):
                        sp.dma_start((Qs, Ks)[w][n * HD:(n + 1) * HD, gn % 2, :,
                                                 half * HALF:(half + 1) * HALF].bitcast(F32),
                                     qk_scratch[unit, part].rearrange("(h c) t -> c h t", h=GH)
                                     ).then_inc(stacked[unit % 2], 16)

                def work(b, items):
                    if b is None:
                        sp.dma_start(w_group[:, 0:4].bitcast(F32), w_scratch[0, :, 0:4]).then_inc(w_qk_in, 16)
                        sp.dma_start(w_group[:, 4:6].bitcast(F32), w_scratch[0, :, 4:6]).then_inc(w_v_in, 16)
                    for kind, g, i, f, high, bnn, ring in items:
                        if kind in F_KINDS:
                            bank, before = fill_no(b, f)
                        next_weights = items is not LAST_ITEMS or g < G - 2
                        if kind == "P" and is_last_piece(kind, i) and i[0] < 4:
                            unit, _, ahead = i
                            w = PROJECTIONS[unit][0]
                            bn_, gn = after(b, g, ahead)
                            if not (b is None and ahead == 1):
                                sp.wait_ge(stacked[unit % 2], per_group(bn_, gn, 2 * UNIT_DMAS,
                                                                        (unit // 2 - 1) * UNIT_DMAS))
                            if g >= 0 and w == 0:
                                taken = GH * (FIRST[1] + TPH) if ahead == 2 else 1
                                sp.wait_ge(scored, per_group(b, g, GH * NS, taken))
                            sp.wait_ge(fill_free[bank], before + 2)
                            sp.dma_start(qk_scratch[unit].rearrange("a p t -> p a t"),
                                         qk_part[:, unit % 2].bitcast(F32)).then_inc(parked[unit % 2], 16)
                            if w == 1:
                                stack_unit((bn_, gn), unit - 1)
                                stack_unit((bn_, gn), unit)
                            if unit == 3 and next_weights:
                                sp.dma_start(w_group[:, 0:4].bitcast(F32),
                                             w_scratch[(g + 2) % G, :, 0:4]).then_inc(w_qk_in, 16)
                        elif kind == "P" and i == (5, PIECES - 1, 1) and next_weights:
                            sp.wait_ge(fill_full, fill_count(b, f))
                            sp.dma_start(w_group[:, 4:6].bitcast(F32),
                                         w_scratch[(g + 2) % G, :, 4:6]).then_inc(w_v_in, 16)
                        elif kind == "C":
                            gn = after(b, g)[1]
                            sp.wait_ge(fill_free[bank], before + 2)
                            for h in range(GH):
                                sp.dma_start(
                                    Qs[KROWS:KROWS + 1, gn % 2, h, :].bitcast(F32).rearrange("p (t q) -> p t q", t=QT),
                                    neg_max[h * QT:(h + 1) * QT, :].bitcast(F32)).then_inc(rows_in, 16)
                        elif kind == "LS" and b is not None:
                            sp.wait_ge(bn_done, bn_count(b, bnn))
                            load_x(b, (i + 2) % QT)
                        elif kind == "LA" and b is not None and i + 2 < QT:
                            sp.wait_ge(x_norm_done, next_batch_tiles(b, i) + 1)
                            load_x(b, i + 2)
                        elif kind == "sc" and g == 0 and i == (0, 0) and items is ITEMS:
                            sp.wait_ge(x_norm_done, b * QT + QT)
                            load_x(b, 0)
                            load_x(b, 1)
                        elif kind == "sc" and g == G - 1 and i == (0, 0):
                            for k in range(4):
                                sp.wait_ge(x2_stored[k], b * 32 + 1)
                                sp.sem_inc(sp_passed, 1)
                            sp.wait_ge(stats_saved, b + 1)
                            for k in range(4):
                                load_residual(b, k)
                        elif kind == "O":
                            sp.wait_ge(x2_done, b * QT + (i + 1))
                            sp.sem_inc(sp_passed, 1)
                            sp.dma_start(x2_scratch[bass.ds(b * QT + i, 1)].rearrange("o p d -> p (o d)"),
                                         x_res[:, i % 4]).then_inc(x2_stored[i % 4], 16)
                            if 1 <= i <= 4:
                                sp.wait_ge(x2_stored[i - 1], b * 32 + 17)
                                sp.sem_inc(sp_passed, 1)
                                sp.wait_ge(x2_stat_done, b * QT + i)
                                load_residual(b, i + 3)
                run(sp, work)
                for k in range(4):
                    sp.wait_ge(x2_stored[k], 32 * B + 1)


def linear_block(nc, sb, pb, sem, x2_scratch, fw_scratch, fw_inverse, ffn_b, out_t, ident_bf, stats_all,
                 rstd_all):
    UT = 2
    UNITS = TILES // UT
    SLOTS = 8
    COLUMNS_DONE = 9
    CLIP_LAG, PRODUCT_LAG, OUT_LAG = 2, 3, 4
    DEEP = 4
    AHEAD = 6
    with ExitStack() as mem:
        w_T = sb(mem, "f_wT", [P, KC, D], BF16)
        bias = sb(mem, "f_bias", [P, D])
        dev = sb(mem, "f_dev", [P, 3, TILES])
        mul_col = sb(mem, "f_mul", [P, TILES])
        add_col = sb(mem, "f_add", [P, TILES])
        part_max = sb(mem, "f_part_max", [P, 1])
        amax = sb(mem, "f_amax", [P, 1])
        scale = sb(mem, "f_scale", [P, 1])
        inverse = sb(mem, "f_inverse", [P, 1])
        back = sb(mem, "f_back", [P, 1])
        x2 = sb(mem, "f_x2", [P, SLOTS, UT, D])
        z = sb(mem, "f_z", [P, DEEP, UT, D])
        power = sb(mem, "f_power", [P, DEEP, UT, D])
        zq = sb(mem, "f_zq", [P, DEEP, UT, D], BF16)
        zT = sb(mem, "f_zT", [P, UT, KC, P], BF16)
        y = sb(mem, "f_y", [P, 2, UT, D], BF16)
        t_bank = pb(mem, "f_t_bank", [P, UT, 2 * HALF], BF16)
        o_bank = pb(mem, "f_o_bank", [P, 2 * UT, D])

        w_in, b_in = sem("f_w_in"), sem("f_b_in")
        small = sem("f_small")
        all_max = sem("f_all_max")
        x2_in = [sem(f"f_x2_in{k}") for k in range(SLOTS)]
        z_done = sem("f_z_done")
        p_done = sem("f_p_done")
        r_done = sem("f_r_done")
        q_done = sem("f_q_done")
        t_full, t_out = sem("f_t_full"), sem("f_t_out")
        o_full, o_out = sem("f_o_full"), sem("f_o_out")
        y_done = sem("f_y_done")
        stored = [sem(f"f_stored{k}") for k in range(SLOTS)]
        sp_passed = sem("f_sp_passed")

        def run(eng, step, lag):
            for k in range(SLOTS):
                step(0, k)
            with eng.Fori(1, UNITS // SLOTS) as i:
                for k in range(SLOTS):
                    step(i, k)
            for k in range(lag):
                step(UNITS // SLOTS, k)

        def number(i, k):
            n = i * SLOTS + k
            return None if isinstance(n, int) and not 0 <= n < UNITS else n

        with nc.Block() as block:
            @block.sync
            def _(sp):
                def load(i, k):
                    sp.sem_inc(sp_passed, 1)
                    sp.dma_start(x2[:, k % SLOTS],
                                 x2_scratch[bass.ds((i * SLOTS + k) * UT, UT)].rearrange("t p d -> p t d")
                                 ).then_inc(x2_in[k % SLOTS], 16)

                def step(i, k):
                    wraps = k >= SLOTS - AHEAD
                    if not (isinstance(i, int) and i == UNITS // SLOTS - 1 and wraps):
                        if not (isinstance(i, int) and i == 0 and not wraps):
                            sp.wait_ge(stored[(k + AHEAD) % SLOTS], i * 16 + 16 * wraps)
                        load(i, k + AHEAD)
                    sp.wait_ge(y_done, i * SLOTS + (k + 1))
                    sp.sem_inc(sp_passed, 1)
                    sp.dma_start(out_t[bass.ds((i * SLOTS + k) * UT, UT)].rearrange("t p d -> p t d"),
                                 x2[:, k]).then_inc(stored[k], 16)
                load(0, 0)
                load(0, 1)
                sp.dma_start(w_T[:], fw_scratch[:]).then_inc(w_in, 16)
                sp.dma_start(bias[:], ffn_b.rearrange("(o n) -> o n", o=1).broadcast_to((P, D))).then_inc(b_in, 16)
                for k in range(2, AHEAD):
                    load(0, k)
                for k in range(SLOTS):
                    step(0, k)
                with sp.Fori(1, UNITS // SLOTS - 1) as i:
                    for k in range(SLOTS):
                        step(i, k)
                for k in range(SLOTS):
                    step(UNITS // SLOTS - 1, k)
                for k in range(SLOTS):
                    sp.wait_ge(stored[k], 16 * UNITS // SLOTS)

            @block.gpsimd
            def _(pool):
                pool.wait_ge(small, 4)
                nc.gpsimd.partition_all_reduce(amax[:], part_max[:], P, RMAX).then_inc(all_max, 1)

                def step(i, k):
                    u = number(i, k)
                    if u is not None:
                        pool.wait_ge(p_done, u * 3 + 3)
                        if not (isinstance(u, int) and u < DEEP):
                            pool.wait_ge(t_full, u * UT - (DEEP - 1) * UT)
                        nc.gpsimd.tensor_tensor(zq[:, k % DEEP], z[:, k % DEEP], power[:, k % DEEP],
                                                ALU.subtract).then_inc(r_done, 1)
                    u = number(i, k - OUT_LAG)
                    if u is not None:
                        pool.wait_ge(o_out, u * UT + UT)
                        slot = x2[:, (k - OUT_LAG) % SLOTS]
                        nc.gpsimd.tensor_tensor(slot, slot, y[:, (k - OUT_LAG) % 2], ALU.add).then_inc(y_done, 1)
                run(pool, step, OUT_LAG)

            @block.vector
            def _(dve):
                done = [0]

                def chained(ins):
                    done[0] += 1
                    ins.then_inc(small, 1)
                    dve.wait_ge(small, done[0])

                mean, largest, least = stats_all[:, :, 0], stats_all[:, :, 2], stats_all[:, :, 3]
                nc.vector.tensor_tensor(dev[:, 0], largest, mean, ALU.subtract)
                chained(nc.vector.tensor_tensor(dev[:, 1], mean, least, ALU.subtract))
                chained(nc.vector.tensor_tensor(dev[:, 0], dev[:, 0], dev[:, 1], ALU.max))
                chained(nc.vector.tensor_tensor(dev[:, 0], dev[:, 0], rstd_all[:], ALU.mult))
                chained(nc.vector.tensor_reduce(part_max[:], dev[:, 0], AX.X, ALU.max))
                dve.wait_ge(all_max, 1)
                chained(nc.vector.tensor_scalar(amax[:], amax[:], 1e-12, None, ALU.max))
                chained(nc.vector.reciprocal(scale[:], amax[:]))
                chained(nc.vector.tensor_scalar(scale[:], scale[:], FP8_MAX, FP8_MAX, ALU.mult, ALU.min))
                chained(nc.vector.tensor_scalar(mul_col[:], rstd_all[:], scale[:], None, ALU.mult))
                chained(nc.vector.scalar_tensor_tensor(out=add_col[:], in0=mean, scalar=-1.0, in1=mul_col[:],
                                                       op0=ALU.mult, op1=ALU.mult))
                assert done[0] == COLUMNS_DONE
                chained(nc.vector.reciprocal(inverse[:], scale[:]))
                chained(nc.vector.tensor_tensor(back[:], inverse[:], fw_inverse[:], ALU.mult))
                dve.wait_ge(b_in, 16)

                def step(i, k):
                    u = number(i, k)
                    if u is not None:
                        zk = z[:, k % DEEP].rearrange("p t d -> p (t d)")
                        pk = power[:, k % DEEP].rearrange("p t d -> p (t d)")
                        dve.wait_ge(z_done, u + 1)
                        nc.vector.tensor_scalar(pk.bitcast(U32), zk.bitcast(U32), EXPONENT, None,
                                                ALU.bitwise_and).then_inc(p_done, 1)
                        dve.wait_ge(p_done, u * 3 + 1)
                        nc.vector.tensor_scalar(pk, pk, SMALLEST, MAGIC, ALU.max, ALU.mult).then_inc(p_done, 1)
                        dve.wait_ge(p_done, u * 3 + 2)
                        nc.vector.tensor_tensor(zk, zk, pk, ALU.add).then_inc(p_done, 1)
                    u = number(i, k - CLIP_LAG)
                    if u is not None:
                        dve.wait_ge(r_done, u + 1)
                        rounded = zq[:, (k - CLIP_LAG) % DEEP].rearrange("p t d -> p (t d)")
                        nc.vector.tensor_scalar(rounded, rounded, FP8_MAX, -FP8_MAX, ALU.min,
                                                ALU.max).then_inc(q_done, 1)
                    u = number(i, k - OUT_LAG)
                    if u is not None:
                        if not (isinstance(u, int) and u < 2):
                            dve.wait_ge(y_done, u - 1)
                        for t in range(UT):
                            dve.wait_ge(o_full, u * UT + (t + 1))
                            nc.vector.scalar_tensor_tensor(out=y[:, (k - OUT_LAG) % 2, t],
                                                           in0=o_bank[:, (k - OUT_LAG) % 2 * UT + t],
                                                           scalar=back[:], in1=bias[:], op0=ALU.mult,
                                                           op1=ALU.add).then_inc(o_out, 1)
                run(dve, step, OUT_LAG)

            @block.tensor
            def _(pe):
                pe.wait_ge(w_in, 16)

                def step(i, k):
                    u = number(i, k - PRODUCT_LAG)
                    if u is None:
                        return
                    for t in range(UT):
                        if t == 0:
                            pe.wait_ge(q_done, u + 1)
                        if not (isinstance(u, int) and u < 1):
                            pe.wait_ge(t_out, u * UT + (t + 1 - UT))
                        for c in range(KC):
                            last = nc.tensor.transpose(t_bank[:, t, c * P:(c + 1) * P],
                                                       zq[:, (k - PRODUCT_LAG) % DEEP, t, c * P:(c + 1) * P], ident_bf[:])
                        last.then_inc(t_full, 1)
                    for t in range(UT):
                        pe.wait_ge(t_out, u * UT + (t + 1))
                        if not (isinstance(u, int) and u < 2):
                            pe.wait_ge(o_out, u * UT + (t + 1 - 2 * UT))
                        for c in range(KC):
                            last = nc.tensor.matmul(o_bank[:, (k - PRODUCT_LAG) % 2 * UT + t], zT[:, t, c], w_T[:, c],
                                                    start=c == 0, stop=c == KC - 1)
                        last.then_inc(o_full, 1)
                run(pe, step, PRODUCT_LAG)

            @block.scalar
            def _(act):
                def step(i, k):
                    u = number(i, k)
                    if u is not None:
                        act.wait_ge(x2_in[k], i * 16 + 16)
                        if not (isinstance(u, int) and u < DEEP):
                            act.wait_ge(r_done, u - (DEEP - 1))
                        for t in range(UT):
                            col = bass.ds(u * UT + t, 1)
                            last = nc.scalar.activation(z[:, k % DEEP, t], x2[:, k, t], ACT.Identity,
                                                        bias=add_col[:, col], scale=mul_col[:, col])
                        last.then_inc(z_done, 1)
                    u = number(i, k - PRODUCT_LAG)
                    if u is not None:
                        for t in range(UT):
                            act.wait_ge(t_full, u * UT + (t + 1))
                            if not (isinstance(u, int) and u < 1):
                                act.wait_ge(o_full, u * UT + (t + 1 - UT))
                            nc.scalar.activation(zT[:, t].rearrange("p c t -> p (c t)"), t_bank[:, t, 0:D],
                                                 ACT.Copy).then_inc(t_out, 1)
                act.wait_ge(small, COLUMNS_DONE)
                run(act, step, PRODUCT_LAG)


_INS = ["L0_attn_x", "L0_attn_q_proj_weight", "L0_attn_k_proj_weight", "L0_attn_v_proj_weight",
        "L0_attn_o_proj_weight", "L0_ffn_weight", "L0_ffn_bias"]


def kernel(**inputs):
    import numpy as _np
    import concourse.bacc as _bacc
    from concourse.bass_utils import run_bass_kernel_spmd as _run

    nc = _bacc.Bacc("TRN2", target_bir_lowering=False, num_devices=1)
    arrays, args = {}, []
    for name in _INS:
        a = _np.ascontiguousarray(inputs[name])
        arrays[f"in_{name}"] = a
        args.append(nc.dram_tensor(f"in_{name}", a.shape, mybir.dt.from_np(a.dtype), kind="ExternalInput").ap())
    out = nc.dram_tensor("out_x", (B, S, D), F32, kind="ExternalOutput").ap()
    nc.disable_value_cache = True
    build_kernel(nc, *args, out)
    r = _run(nc, [arrays], core_ids=[0])
    return r.results[0]["out_x"]
```
